# Optimizing a Trainium2 kernel written in Bass

```python
import numpy as np
import jax
import jax.numpy as jnp

def _softmax(x, axis=-1):
    return jax.nn.softmax(x, axis=axis)

def _gelu(x):
    return jax.nn.gelu(x, approximate=True)

def _silu(x):
    return jax.nn.silu(x)

def _sigmoid(x):
    return jax.nn.sigmoid(x)

def _layernorm(x, axis=-1, eps=1e-05):
    m = jnp.mean(x, axis=axis, keepdims=True)
    v = jnp.var(x, axis=axis, keepdims=True)
    return (x - m) / jnp.sqrt(v + eps)

def _scatter_add(tgt, idx, src, axis=0):
    return tgt.at[idx].add(src)

def _segment_sum(src, seg, n):
    return jax.ops.segment_sum(src, seg, n)
kernel_name = 'mk_xattn_ffn_d4_seqx_r8_7ae67a'

def setup_inputs(seed: int=0):
    np.random.seed(seed)
    _w = jnp.asarray

    def _rec_inputs():
        import jax
        import jax.numpy as jnp
        _rk = jax.random.key(seed)
        x = -0.0002928 + 1 * jax.random.normal(jax.random.fold_in(_rk, 1), (8, 256, 128), jnp.float32)
        _lenS = 256 - jax.random.randint(jax.random.fold_in(_rk, 7), (8,), 0, max(1, 256 // 4) + 1, jnp.int32)
        _lenS2 = 256 - jax.random.randint(jax.random.fold_in(_rk, 8), (8,), 0, max(1, 256 // 4) + 1, jnp.int32)
        _ctx_1024P = jax.random.normal(jax.random.fold_in(_rk, 11), (8, 16, 128), jnp.float32)
        _ctx_1024c = jax.random.dirichlet(jax.random.fold_in(_rk, 511), 0.3 * jnp.ones((16,), jnp.float32), (8, 256))
        _ctx_1024t = jnp.einsum('bsk,bkd->bsd', _ctx_1024c, _ctx_1024P)
        _ctx_1024t = _ctx_1024t * jax.lax.rsqrt(jnp.mean(jnp.square(_ctx_1024t)) + 1e-12) * 0.953939
        ctx_1024 = -1.39393e-06 + 0.999914 * (_ctx_1024t + 0.3 * jax.random.normal(jax.random.fold_in(_rk, 611), (8, 256, 128), jnp.float32))
        fside_BxSxS2_0 = -0.000354355 + 1.00006 * jax.random.normal(jax.random.fold_in(_rk, 14), (8, 256, 256), jnp.float32)
        _validS = jnp.arange(256)[None, :] < _lenS[:, None]
        _validS2 = jnp.arange(256)[None, :] < _lenS2[:, None]
        _causal = jnp.tril(jnp.ones((256, 256), dtype=bool))
        mask_BxSxS2_bk0 = jnp.logical_not(jnp.broadcast_to(_validS2[:, None, :], (8, 256, 256)))
        mask_Bx1xSxS2_ik1 = jnp.where(jnp.broadcast_to(_validS2[:, None, None, :], (8, 1, 256, 256)), 1, 0).astype(jnp.int32)
        mask_Bx1xSxS2_if1 = jnp.where(jnp.ones((8, 1, 256, 256), dtype=bool), 1, 0).astype(jnp.int32)
        return (x, ctx_1024, fside_BxSxS2_0, mask_BxSxS2_bk0, mask_Bx1xSxS2_ik1, mask_Bx1xSxS2_if1)
    x, ctx_1024, fside_BxSxS2_0, mask_BxSxS2_bk0, mask_Bx1xSxS2_ik1, mask_Bx1xSxS2_if1 = _rec_inputs()

    def _L0_xattn_setup():
        import jax, jax.numpy as jnp
        import numpy as np
        B, LQ, LK, D, H, DH = (2, 256, 256, 128, 16, 64)
        INIT_STD = 0.02
        key = jax.random.key(seed)
        ks = jax.random.split(key, 8)
        query = jax.random.normal(ks[0], (B, LQ, D), dtype=jnp.float32)
        key_value = jax.random.normal(ks[1], (B, LK, D), dtype=jnp.float32)
        mask = jax.random.randint(ks[2], (B, LQ, LK), 0, 2) > 0
        position_bias = jax.random.normal(ks[3], (H, LQ, LK), dtype=jnp.float32)
        Wq = jax.random.normal(ks[4], (H * DH, D), dtype=jnp.float32) * INIT_STD
        Wk = jax.random.normal(ks[5], (H * DH, D), dtype=jnp.float32) * INIT_STD
        Wv = jax.random.normal(ks[6], (H * DH, D), dtype=jnp.float32) * INIT_STD
        Wo = jax.random.normal(ks[7], (D, H * DH), dtype=jnp.float32) * INIT_STD
        return {'query': query, 'key_value': key_value, 'mask': mask, 'position_bias': position_bias, 'Wq': Wq, 'Wk': Wk, 'Wv': Wv, 'Wo': Wo}
    _L0_xattn_all = _L0_xattn_setup()
    _L0_xattn_in = {k: v for k, v in _L0_xattn_all.items() if k in ('position_bias', 'Wq', 'Wk', 'Wv', 'Wo')}
    del _L0_xattn_all

    def _L0_ffn_setup():
        import jax, jax.numpy as jnp
        import numpy as np
        B, L, D = (4, 64, 128)
        E, TOP_K = (16, 4)
        F = 4 * D
        key = jax.random.key(seed)
        ks = jax.random.split(key, 6)
        scale = 0.02
        return {'x': jax.random.normal(ks[0], (B, L, D), jnp.float32), 'keys': jax.random.normal(ks[1], (E, D), jnp.float32), 'w1': jax.random.normal(ks[2], (E, F, D), jnp.float32) * scale, 'b1': jnp.zeros((E, F), jnp.float32), 'w2': jax.random.normal(ks[3], (E, D, F), jnp.float32) * scale, 'b2': jnp.zeros((E, D), jnp.float32), 'rw': jax.random.normal(ks[4], (E, D), jnp.float32) * scale, 'rb': jnp.zeros((E,), jnp.float32)}
    _L0_ffn_all = _L0_ffn_setup()
    _L0_ffn_in = {k: v for k, v in _L0_ffn_all.items() if k in ('keys', 'w1', 'b1', 'w2', 'b2', 'rw', 'rb')}
    del _L0_ffn_all

    def _L1_xattn_setup():
        import jax, jax.numpy as jnp
        import numpy as np
        D_MODEL = 128
        N_HEADS = 16
        D_HEAD = D_MODEL // N_HEADS
        SCALE = float(np.sqrt(D_HEAD))
        key = jax.random.key(seed)
        ks = jax.random.split(key, 16)
        B, S, D = (2, 256, D_MODEL)
        s = 1.0 / np.sqrt(D)
        inp = {'query': jax.random.normal(ks[0], (B, S, D), jnp.float32), 'key': jax.random.normal(ks[1], (B, S, D), jnp.float32), 'value': jax.random.normal(ks[2], (B, S, D), jnp.float32), 'mask': jax.random.randint(ks[3], (B, 1, S, S), 0, 2, jnp.int32), 'chemical_bias': jax.random.normal(ks[4], (B, S, S), jnp.float32), 'Wq': jax.random.normal(ks[5], (D, D), jnp.float32) * s, 'bq': jax.random.normal(ks[6], (D,), jnp.float32) * s, 'Wk': jax.random.normal(ks[7], (D, D), jnp.float32) * s, 'bk': jax.random.normal(ks[8], (D,), jnp.float32) * s, 'Wv': jax.random.normal(ks[9], (D, D), jnp.float32) * s, 'bv': jax.random.normal(ks[10], (D,), jnp.float32) * s, 'Wo': jax.random.normal(ks[11], (D, D), jnp.float32) * s, 'bo': jax.random.normal(ks[12], (D,), jnp.float32) * s}
        return inp
    _L1_xattn_all = _L1_xattn_setup()
    _L1_xattn_in = {k: v for k, v in _L1_xattn_all.items() if k in ('Wq', 'bq', 'Wk', 'bk', 'Wv', 'bv', 'Wo', 'bo')}
    del _L1_xattn_all

    def _L1_ffn_setup():
        import jax, jax.numpy as jnp
        import numpy as np
        H = 128
        I = 64
        E = 8
        K = 2
        SI = I * 2
        B, S = (2, 128)

        def _mlp(x, gw, uw, dw):
            return jax.nn.silu(x @ gw.T) * (x @ uw.T) @ dw.T
        key = jax.random.key(seed)
        ks = jax.random.split(key, 9)
        s = 0.02
        return {'x': jax.random.normal(ks[0], (B, S, H), jnp.float32), 'gate_w': jax.random.normal(ks[1], (E, H), jnp.float32) * s, 'lb_bias': jnp.zeros((E,), jnp.float32), 'expert_gate_w': jax.random.normal(ks[2], (E, I, H), jnp.float32) * s, 'expert_up_w': jax.random.normal(ks[3], (E, I, H), jnp.float32) * s, 'expert_down_w': jax.random.normal(ks[4], (E, H, I), jnp.float32) * s, 'shared_gate_w': jax.random.normal(ks[5], (SI, H), jnp.float32) * s, 'shared_up_w': jax.random.normal(ks[6], (SI, H), jnp.float32) * s, 'shared_down_w': jax.random.normal(ks[7], (H, SI), jnp.float32) * s}
    _L1_ffn_all = _L1_ffn_setup()
    _L1_ffn_in = {k: v for k, v in _L1_ffn_all.items() if k in ('gate_w', 'lb_bias', 'expert_gate_w', 'expert_up_w', 'expert_down_w', 'shared_gate_w', 'shared_up_w', 'shared_down_w')}
    del _L1_ffn_all

    def _L2_xattn_setup():
        import jax, jax.numpy as jnp
        import numpy as np
        import math
        HIDDEN = 128
        HEADS = 16
        HEAD = HIDDEN // HEADS
        SCALE_BASE = 512.0

        def _gammas(heads):
            return 1.0 - jnp.exp(jnp.linspace(math.log(1.0 / 32.0), math.log(1.0 / 512.0), heads))

        def _xpos(x, downscale):
            S, d = (x.shape[2], x.shape[3])
            half = d // 2
            base_scale = (jnp.arange(0, d, 2, dtype=jnp.float32) + 0.4 * d) / (1.4 * d)
            pos = jnp.arange(S, dtype=jnp.float32)
            scale = base_scale[None, :] ** (pos / SCALE_BASE)[:, None]
            if downscale:
                scale = 1.0 / scale
            inv_freq = 1.0 / 10000.0 ** (jnp.arange(half, dtype=jnp.float32) / half)
            sinusoid = pos[:, None] * inv_freq[None, :]
            sin = jnp.repeat(jnp.sin(sinusoid) * scale, 2, axis=-1)
            cos = jnp.repeat(jnp.cos(sinusoid) * scale, 2, axis=-1)
            x1 = x[..., ::2]
            x2 = x[..., 1::2]
            rot = jnp.stack([-x2, x1], axis=-1).reshape(x.shape)
            return x * cos + rot * sin

        def _decay_mask(S, gammas):
            n = jnp.arange(S)[:, None]
            m = jnp.arange(S)[None, :]
            diff = (n - m).astype(jnp.float32)
            mask = n >= m
            pw = jnp.maximum(diff, 0.0)[None, :, :]
            return jnp.where(mask[None, :, :], gammas[:, None, None] ** pw, 0.0)

        def retention_forward(Q, K, V):
            B, S, _ = Q.shape

            def split(x, hd):
                return x.reshape(B, S, HEADS, hd).transpose(0, 2, 1, 3)
            q = _xpos(split(Q, HEAD), downscale=False)
            k = _xpos(split(K, HEAD), downscale=True)
            v = split(V, HEAD)
            D = _decay_mask(S, _gammas(HEADS).astype(Q.dtype))
            scores = jnp.einsum('bhsd,bhtd->bhst', q, k) * D[None]
            out = jnp.einsum('bhst,bhtd->bhsd', scores, v)
            return out.transpose(0, 2, 1, 3).reshape(B, S, HEADS * HEAD)
        key = jax.random.key(seed)
        kq, kk, kv = jax.random.split(key, 3)
        B, S = (2, 256)
        return {'Q': jax.random.normal(kq, (B, S, HIDDEN), dtype=jnp.float32), 'K': jax.random.normal(kk, (B, S, HIDDEN), dtype=jnp.float32), 'V': jax.random.normal(kv, (B, S, HIDDEN), dtype=jnp.float32)}
    _L2_xattn_all = _L2_xattn_setup()
    _L2_xattn_in = {k: v for k, v in _L2_xattn_all.items() if k in ()}
    del _L2_xattn_all

    def _L2_ffn_setup():
        import jax, jax.numpy as jnp
        import numpy as np
        TOP_K = 2
        key = jax.random.key(seed)
        ks = jax.random.split(key, 7)
        B, L, D, H, E, S = (2, 256, 128, 64, 16, 256)
        s = lambda fan_in: (1.0 / np.sqrt(fan_in)).astype(np.float32)
        return {'x': jax.random.normal(ks[0], (B, L, D), jnp.float32), 'gate_w': jax.random.normal(ks[1], (E, D), jnp.float32) * s(D), 'w1': jax.random.normal(ks[2], (E, H, D), jnp.float32) * s(D), 'w2': jax.random.normal(ks[3], (E, D, H), jnp.float32) * s(H), 'sfc1': jax.random.normal(ks[4], (S, D), jnp.float32) * s(D), 'sfc2': jax.random.normal(ks[5], (S, D), jnp.float32) * s(D), 'sfc3': jax.random.normal(ks[6], (D, S), jnp.float32) * s(S)}
    _L2_ffn_all = _L2_ffn_setup()
    _L2_ffn_in = {k: v for k, v in _L2_ffn_all.items() if k in ('gate_w', 'w1', 'w2', 'sfc1', 'sfc2', 'sfc3')}
    del _L2_ffn_all

    def _L3_xattn_setup():
        import jax, jax.numpy as jnp
        import numpy as np
        D_MODEL = 128
        H = 16
        D_K = D_MODEL // H
        key = jax.random.key(seed)
        ks = jax.random.split(key, 12)
        B, S = (4, 256)
        scale = 1.0 / np.sqrt(D_MODEL)
        inp = {'query': jax.random.normal(ks[0], (B, S, D_MODEL), jnp.float32), 'key': jax.random.normal(ks[1], (B, S, D_MODEL), jnp.float32), 'value': jax.random.normal(ks[2], (B, S, D_MODEL), jnp.float32), 'mask': jnp.ones((B, 1, S, S), jnp.int32), 'Wq': jax.random.normal(ks[3], (D_MODEL, D_MODEL), jnp.float32) * scale, 'bq': jnp.zeros((D_MODEL,), jnp.float32), 'Wk': jax.random.normal(ks[4], (D_MODEL, D_MODEL), jnp.float32) * scale, 'bk': jnp.zeros((D_MODEL,), jnp.float32), 'Wv': jax.random.normal(ks[5], (D_MODEL, D_MODEL), jnp.float32) * scale, 'bv': jnp.zeros((D_MODEL,), jnp.float32), 'Wo': jax.random.normal(ks[6], (D_MODEL, D_MODEL), jnp.float32) * scale, 'bo': jnp.zeros((D_MODEL,), jnp.float32)}
        return inp
    _L3_xattn_all = _L3_xattn_setup()
    _L3_xattn_in = {k: v for k, v in _L3_xattn_all.items() if k in ('Wq', 'bq', 'Wk', 'bk', 'Wv', 'bv', 'Wo', 'bo')}
    del _L3_xattn_all

    def _L3_ffn_setup():
        import jax, jax.numpy as jnp
        import numpy as np

        def _bitlinear(x, w_latent):
            scale = jax.lax.stop_gradient(jnp.clip(jnp.mean(jnp.abs(w_latent), axis=1, keepdims=True), 1e-05, None))
            tern = jnp.clip(jnp.round(w_latent / scale), -1.0, 1.0)
            w = w_latent + jax.lax.stop_gradient(tern - w_latent)
            return x @ (w * scale).T
        key = jax.random.key(seed)
        ks = jax.random.split(key, 6)
        dim, hidden, rank = (128, 512, 16)
        B, S = (4, 512)
        x = jax.random.normal(ks[0], (B, S, dim), dtype=jnp.float32)
        w_fc = 0.02 * jax.random.normal(ks[1], (hidden, dim), dtype=jnp.float32)
        w_proj = 0.02 * jax.random.normal(ks[2], (dim, hidden), dtype=jnp.float32)
        u = 0.02 * jax.random.normal(ks[3], (hidden, rank), dtype=jnp.float32)
        v = 0.02 * jax.random.normal(ks[4], (rank, dim), dtype=jnp.float32)
        fast_b = jax.random.normal(ks[5], (rank, rank), dtype=jnp.float32)
        gate = jnp.float32(0.05)
        return {'x': x, 'fast_b': fast_b, 'w_fc': w_fc, 'w_proj': w_proj, 'u': u, 'v': v, 'gate': gate}
    _L3_ffn_all = _L3_ffn_setup()
    _L3_ffn_in = {k: v for k, v in _L3_ffn_all.items() if k in ('fast_b', 'w_fc', 'w_proj', 'u', 'v', 'gate')}
    del _L3_ffn_all
    return {'x': x, 'ctx_1024': ctx_1024, 'fside_BxSxS2_0': fside_BxSxS2_0, 'mask_BxSxS2_bk0': mask_BxSxS2_bk0, 'mask_Bx1xSxS2_ik1': mask_Bx1xSxS2_ik1, 'mask_Bx1xSxS2_if1': mask_Bx1xSxS2_if1, 'L0_xattn_position_bias': _L0_xattn_in['position_bias'], 'L0_xattn_Wq': _L0_xattn_in['Wq'], 'L0_xattn_Wk': _L0_xattn_in['Wk'], 'L0_xattn_Wv': _L0_xattn_in['Wv'], 'L0_xattn_Wo': _L0_xattn_in['Wo'], 'L0_ffn_keys': _L0_ffn_in['keys'], 'L0_ffn_w1': _L0_ffn_in['w1'], 'L0_ffn_b1': _L0_ffn_in['b1'], 'L0_ffn_w2': _L0_ffn_in['w2'], 'L0_ffn_b2': _L0_ffn_in['b2'], 'L0_ffn_rw': _L0_ffn_in['rw'], 'L0_ffn_rb': _L0_ffn_in['rb'], 'L1_xattn_Wq': _L1_xattn_in['Wq'], 'L1_xattn_bq': _L1_xattn_in['bq'], 'L1_xattn_Wk': _L1_xattn_in['Wk'], 'L1_xattn_bk': _L1_xattn_in['bk'], 'L1_xattn_Wv': _L1_xattn_in['Wv'], 'L1_xattn_bv': _L1_xattn_in['bv'], 'L1_xattn_Wo': _L1_xattn_in['Wo'], 'L1_xattn_bo': _L1_xattn_in['bo'], 'L1_ffn_gate_w': _L1_ffn_in['gate_w'], 'L1_ffn_lb_bias': _L1_ffn_in['lb_bias'], 'L1_ffn_expert_gate_w': _L1_ffn_in['expert_gate_w'], 'L1_ffn_expert_up_w': _L1_ffn_in['expert_up_w'], 'L1_ffn_expert_down_w': _L1_ffn_in['expert_down_w'], 'L1_ffn_shared_gate_w': _L1_ffn_in['shared_gate_w'], 'L1_ffn_shared_up_w': _L1_ffn_in['shared_up_w'], 'L1_ffn_shared_down_w': _L1_ffn_in['shared_down_w'], 'L2_ffn_gate_w': _L2_ffn_in['gate_w'], 'L2_ffn_w1': _L2_ffn_in['w1'], 'L2_ffn_w2': _L2_ffn_in['w2'], 'L2_ffn_sfc1': _L2_ffn_in['sfc1'], 'L2_ffn_sfc2': _L2_ffn_in['sfc2'], 'L2_ffn_sfc3': _L2_ffn_in['sfc3'], 'L3_xattn_Wq': _L3_xattn_in['Wq'], 'L3_xattn_bq': _L3_xattn_in['bq'], 'L3_xattn_Wk': _L3_xattn_in['Wk'], 'L3_xattn_bk': _L3_xattn_in['bk'], 'L3_xattn_Wv': _L3_xattn_in['Wv'], 'L3_xattn_bv': _L3_xattn_in['bv'], 'L3_xattn_Wo': _L3_xattn_in['Wo'], 'L3_xattn_bo': _L3_xattn_in['bo'], 'L3_ffn_fast_b': _L3_ffn_in['fast_b'], 'L3_ffn_w_fc': _L3_ffn_in['w_fc'], 'L3_ffn_w_proj': _L3_ffn_in['w_proj'], 'L3_ffn_u': _L3_ffn_in['u'], 'L3_ffn_v': _L3_ffn_in['v'], 'L3_ffn_gate': _L3_ffn_in['gate']}

def reference(x, ctx_1024, fside_BxSxS2_0, mask_BxSxS2_bk0, mask_Bx1xSxS2_ik1, mask_Bx1xSxS2_if1, L0_xattn_position_bias, L0_xattn_Wq, L0_xattn_Wk, L0_xattn_Wv, L0_xattn_Wo, L0_ffn_keys, L0_ffn_w1, L0_ffn_b1, L0_ffn_w2, L0_ffn_b2, L0_ffn_rw, L0_ffn_rb, L1_xattn_Wq, L1_xattn_bq, L1_xattn_Wk, L1_xattn_bk, L1_xattn_Wv, L1_xattn_bv, L1_xattn_Wo, L1_xattn_bo, L1_ffn_gate_w, L1_ffn_lb_bias, L1_ffn_expert_gate_w, L1_ffn_expert_up_w, L1_ffn_expert_down_w, L1_ffn_shared_gate_w, L1_ffn_shared_up_w, L1_ffn_shared_down_w, L2_ffn_gate_w, L2_ffn_w1, L2_ffn_w2, L2_ffn_sfc1, L2_ffn_sfc2, L2_ffn_sfc3, L3_xattn_Wq, L3_xattn_bq, L3_xattn_Wk, L3_xattn_bk, L3_xattn_Wv, L3_xattn_bv, L3_xattn_Wo, L3_xattn_bo, L3_ffn_fast_b, L3_ffn_w_fc, L3_ffn_w_proj, L3_ffn_u, L3_ffn_v, L3_ffn_gate):
    import jax
    import jax.numpy as jnp

    def _L0_xattn_ref(query, key_value, mask, position_bias, Wq, Wk, Wv, Wo):
        import jax, jax.numpy as jnp
        import numpy as np
        B, LQ, LK, D, H, DH = (2, 256, 256, 128, 16, 64)
        INIT_STD = 0.02
        b, lq, _ = query.shape
        lk = key_value.shape[1]
        hq = (query @ Wq.T).reshape(b, lq, H, DH).transpose(0, 2, 1, 3)
        hk = (key_value @ Wk.T).reshape(b, lk, H, DH).transpose(0, 2, 1, 3)
        hv = (key_value @ Wv.T).reshape(b, lk, H, DH).transpose(0, 2, 1, 3)
        score = jnp.einsum('bhqd,bhkd->bhqk', hq, hk) / np.float32(np.sqrt(DH))
        score = score + position_bias[None]
        m = mask[:, None]
        score = jnp.where(m, score, jnp.float32(-jnp.inf))
        probs = jax.nn.softmax(score, axis=-1)
        probs = jnp.where(m, probs, jnp.float32(0))
        ctx = jnp.einsum('bhqk,bhkd->bhqd', probs, hv)
        ctx = ctx.transpose(0, 2, 1, 3).reshape(b, lq, H * DH)
        out = ctx @ Wo.T
        return out

    def _L0_ffn_ref(x, keys, w1, b1, w2, b2, rw, rb):
        import jax, jax.numpy as jnp
        import numpy as np
        B, L, D = (4, 64, 128)
        E, TOP_K = (16, 4)
        F = 4 * D
        diff = x[:, :, None, :] - keys
        dist2 = jnp.sum(diff * diff, axis=-1)
        logits = -dist2 + jnp.einsum('bld,ed->ble', x, rw) + rb
        topv, topi = jax.lax.top_k(logits, TOP_K)
        w = jax.nn.softmax(topv, axis=-1)
        hidden = jax.nn.gelu(jnp.einsum('bld,efd->blef', x, w1) + b1, approximate=False)
        exp_out = jnp.einsum('blef,edf->bled', hidden, w2) + b2
        sel = jnp.take_along_axis(exp_out, topi[..., None], axis=2)
        fused = jnp.sum(w[..., None] * sel, axis=2)
        return fused

    def _L1_xattn_ref(query, key, value, mask, chemical_bias, Wq, bq, Wk, bk, Wv, bv, Wo, bo):
        import jax, jax.numpy as jnp
        import numpy as np
        D_MODEL = 128
        N_HEADS = 16
        D_HEAD = D_MODEL // N_HEADS
        SCALE = float(np.sqrt(D_HEAD))
        B, S, D = query.shape
        H, dh = (N_HEADS, D_HEAD)
        q = (query @ Wq.T + bq).reshape(B, S, H, dh).transpose(0, 2, 1, 3)
        k = (key @ Wk.T + bk).reshape(B, S, H, dh).transpose(0, 2, 1, 3)
        v = (value @ Wv.T + bv).reshape(B, S, H, dh).transpose(0, 2, 1, 3)
        scores = jnp.einsum('bhqd,bhkd->bhqk', q, k) / SCALE
        scores = scores + chemical_bias[:, None, :, :]
        scores = jnp.where(mask == 0, -jnp.inf, scores)
        attn = jax.nn.softmax(scores, axis=-1)
        out = jnp.einsum('bhqk,bhkd->bhqd', attn, v)
        out = out.transpose(0, 2, 1, 3).reshape(B, S, D)
        return out @ Wo.T + bo

    def _L1_ffn_ref(x, gate_w, lb_bias, expert_gate_w, expert_up_w, expert_down_w, shared_gate_w, shared_up_w, shared_down_w):
        import jax, jax.numpy as jnp
        import numpy as np
        H = 128
        I = 64
        E = 8
        K = 2
        SI = I * 2
        B, S = (2, 128)

        def _mlp(x, gw, uw, dw):
            return jax.nn.silu(x @ gw.T) * (x @ uw.T) @ dw.T
        b, s, h = x.shape
        xf = x.reshape(-1, h)
        logits = xf @ gate_w.T + lb_bias
        scores = jax.nn.sigmoid(logits.astype(jnp.float32))
        topw, topi = jax.lax.top_k(scores, K)
        topw = (topw / (topw.sum(-1, keepdims=True) + 1e-08)).astype(x.dtype)
        out = jnp.zeros_like(xf)
        for e in range(E):
            m = topi == e
            sel = m.any(axis=-1)
            cnt = m.sum()
            wmean = (topw * m).sum() / jnp.maximum(cnt, 1).astype(topw.dtype)
            y = _mlp(xf, expert_gate_w[e], expert_up_w[e], expert_down_w[e])
            out = out + jnp.where(sel[:, None], y * wmean, jnp.zeros((), x.dtype))
        out = out.reshape(b, s, h)
        out = out + _mlp(x, shared_gate_w, shared_up_w, shared_down_w)
        return out

    def _L2_xattn_ref(Q, K, V):
        import jax, jax.numpy as jnp
        import numpy as np
        import math
        HIDDEN = 128
        HEADS = 16
        HEAD = HIDDEN // HEADS
        SCALE_BASE = 512.0

        def _gammas(heads):
            return 1.0 - jnp.exp(jnp.linspace(math.log(1.0 / 32.0), math.log(1.0 / 512.0), heads))

        def _xpos(x, downscale):
            S, d = (x.shape[2], x.shape[3])
            half = d // 2
            base_scale = (jnp.arange(0, d, 2, dtype=jnp.float32) + 0.4 * d) / (1.4 * d)
            pos = jnp.arange(S, dtype=jnp.float32)
            scale = base_scale[None, :] ** (pos / SCALE_BASE)[:, None]
            if downscale:
                scale = 1.0 / scale
            inv_freq = 1.0 / 10000.0 ** (jnp.arange(half, dtype=jnp.float32) / half)
            sinusoid = pos[:, None] * inv_freq[None, :]
            sin = jnp.repeat(jnp.sin(sinusoid) * scale, 2, axis=-1)
            cos = jnp.repeat(jnp.cos(sinusoid) * scale, 2, axis=-1)
            x1 = x[..., ::2]
            x2 = x[..., 1::2]
            rot = jnp.stack([-x2, x1], axis=-1).reshape(x.shape)
            return x * cos + rot * sin

        def _decay_mask(S, gammas):
            n = jnp.arange(S)[:, None]
            m = jnp.arange(S)[None, :]
            diff = (n - m).astype(jnp.float32)
            mask = n >= m
            pw = jnp.maximum(diff, 0.0)[None, :, :]
            return jnp.where(mask[None, :, :], gammas[:, None, None] ** pw, 0.0)

        def retention_forward(Q, K, V):
            B, S, _ = Q.shape

            def split(x, hd):
                return x.reshape(B, S, HEADS, hd).transpose(0, 2, 1, 3)
            q = _xpos(split(Q, HEAD), downscale=False)
            k = _xpos(split(K, HEAD), downscale=True)
            v = split(V, HEAD)
            D = _decay_mask(S, _gammas(HEADS).astype(Q.dtype))
            scores = jnp.einsum('bhsd,bhtd->bhst', q, k) * D[None]
            out = jnp.einsum('bhst,bhtd->bhsd', scores, v)
            return out.transpose(0, 2, 1, 3).reshape(B, S, HEADS * HEAD)
        return retention_forward(Q, K, V)

    def _L2_ffn_ref(x, gate_w, w1, w2, sfc1, sfc2, sfc3):
        import jax, jax.numpy as jnp
        import numpy as np
        TOP_K = 2
        B, L, D = x.shape
        E = gate_w.shape[0]
        shared = jnp.einsum('bls,ds->bld', jax.nn.silu(jnp.einsum('bld,sd->bls', x, sfc1)) * jnp.einsum('bld,sd->bls', x, sfc2), sfc3)
        logits = jnp.einsum('bld,ed->ble', x, gate_w)
        top_w, top_idx = jax.lax.top_k(logits, TOP_K)
        top_w = jax.nn.softmax(top_w, axis=-1)
        xf = x.reshape(-1, D)
        T = xf.shape[0]
        idx = top_idx.reshape(T, TOP_K)
        wk = top_w.reshape(T, TOP_K)
        dispatch = jnp.zeros((T, E), xf.dtype).at[jnp.arange(T)[:, None], idx].add(wk)
        h = jax.nn.silu(jnp.einsum('td,ehd->teh', xf, w1))
        moe = jnp.einsum('teh,te,edh->td', h, dispatch, w2)
        return moe.reshape(B, L, D) + shared

    def _L3_xattn_ref(query, key, value, mask, Wq, bq, Wk, bk, Wv, bv, Wo, bo):
        import jax, jax.numpy as jnp
        import numpy as np
        D_MODEL = 128
        H = 16
        D_K = D_MODEL // H
        B, S, _ = query.shape
        q = query @ Wq.T + bq
        k = key @ Wk.T + bk
        v = value @ Wv.T + bv
        q = q.reshape(B, S, H, D_K).transpose(0, 2, 1, 3)
        k = k.reshape(B, S, H, D_K).transpose(0, 2, 1, 3)
        v = v.reshape(B, S, H, D_K).transpose(0, 2, 1, 3)
        scores = jnp.einsum('bhsd,bhtd->bhst', q, k) / jnp.sqrt(jnp.asarray(D_K, q.dtype))
        attn = jax.nn.softmax(scores, axis=-1)
        ctx = jnp.einsum('bhst,bhtd->bhsd', attn, v)
        ctx = ctx.transpose(0, 2, 1, 3).reshape(B, S, H * D_K)
        return ctx @ Wo.T + bo

    def _L3_ffn_ref(x, fast_b, w_fc, w_proj, u, v, gate):
        import jax, jax.numpy as jnp
        import numpy as np

        def _bitlinear(x, w_latent):
            scale = jax.lax.stop_gradient(jnp.clip(jnp.mean(jnp.abs(w_latent), axis=1, keepdims=True), 1e-05, None))
            tern = jnp.clip(jnp.round(w_latent / scale), -1.0, 1.0)
            w = w_latent + jax.lax.stop_gradient(tern - w_latent)
            return x @ (w * scale).T
        h = _bitlinear(x, w_fc) + gate * (x @ v.T @ fast_b.T @ u.T)
        r = jnp.maximum(h, 0.0)
        return _bitlinear(r * r, w_proj)
    x = x + _L0_xattn_ref(_layernorm(x, axis=-1), ctx_1024, mask_BxSxS2_bk0, L0_xattn_position_bias, L0_xattn_Wq, L0_xattn_Wk, L0_xattn_Wv, L0_xattn_Wo)
    x = x + _L0_ffn_ref(_layernorm(x, axis=-1), L0_ffn_keys, L0_ffn_w1, L0_ffn_b1, L0_ffn_w2, L0_ffn_b2, L0_ffn_rw, L0_ffn_rb)
    x = x + _L1_xattn_ref(_layernorm(x, axis=-1), ctx_1024, ctx_1024, mask_Bx1xSxS2_ik1, fside_BxSxS2_0, L1_xattn_Wq, L1_xattn_bq, L1_xattn_Wk, L1_xattn_bk, L1_xattn_Wv, L1_xattn_bv, L1_xattn_Wo, L1_xattn_bo)
    x = x + _L1_ffn_ref(_layernorm(x, axis=-1), L1_ffn_gate_w, L1_ffn_lb_bias, L1_ffn_expert_gate_w, L1_ffn_expert_up_w, L1_ffn_expert_down_w, L1_ffn_shared_gate_w, L1_ffn_shared_up_w, L1_ffn_shared_down_w)
    x = x + _L2_xattn_ref(_layernorm(x, axis=-1), ctx_1024, ctx_1024)
    x = x + _L2_ffn_ref(_layernorm(x, axis=-1), L2_ffn_gate_w, L2_ffn_w1, L2_ffn_w2, L2_ffn_sfc1, L2_ffn_sfc2, L2_ffn_sfc3)
    x = x + _L3_xattn_ref(_layernorm(x, axis=-1), ctx_1024, ctx_1024, mask_Bx1xSxS2_if1, L3_xattn_Wq, L3_xattn_bq, L3_xattn_Wk, L3_xattn_bk, L3_xattn_Wv, L3_xattn_bv, L3_xattn_Wo, L3_xattn_bo)
    x = x + _L3_ffn_ref(_layernorm(x, axis=-1), L3_ffn_fast_b, L3_ffn_w_fc, L3_ffn_w_proj, L3_ffn_u, L3_ffn_v, L3_ffn_gate)
    return x

_drawn_inputs = setup_inputs


def setup_inputs(seed=0):
    import zlib

    import numpy as np

    out = dict(_drawn_inputs(seed))
    spreads = {'L0_ffn_b1': (0.0, 0.376),
     'L0_ffn_b2': (0.0, 0.1),
     'L0_ffn_rb': (0.0, 0.8),
     'L1_ffn_lb_bias': (0.0, 0.8),
     'L3_xattn_bq': (0.0, 0.8),
     'L3_xattn_bk': (0.0, 2.0),
     'L3_xattn_bv': (0.0, 2.0),
     'L3_xattn_bo': (0.0, 2.0)}
    factors = {'L0_xattn_Wq': 8.0,
     'L0_xattn_Wk': 8.0,
     'L0_ffn_rw': 8.0,
     'L1_xattn_bk': 64.0,
     'L1_ffn_gate_w': 8.0,
     'L1_ffn_expert_gate_w': 8.0,
     'L1_ffn_expert_up_w': 8.0,
     'L1_ffn_expert_down_w': 8.0,
     'L1_ffn_shared_gate_w': 8.0,
     'L1_ffn_shared_up_w': 8.0,
     'L1_ffn_shared_down_w': 8.0,
     'L2_ffn_gate_w': 8.0,
     'L2_ffn_w1': 8.0,
     'L2_ffn_w2': 8.0,
     'L2_ffn_sfc1': 7.805,
     'L2_ffn_sfc2': 7.123,
     'L2_ffn_sfc3': 7.196,
     'L3_xattn_Wq': 8.0,
     'L3_xattn_Wk': 8.0,
     'L3_xattn_Wv': 7.825,
     'L3_xattn_Wo': 8.0,
     'L3_ffn_fast_b': 8.0,
     'L3_ffn_w_fc': 8.0,
     'L3_ffn_w_proj': 8.0,
     'L3_ffn_u': 8.0,
     'L3_ffn_v': 8.0}
    for name, (base, spread) in spreads.items():
        noise = np.random.default_rng([zlib.crc32(name.encode()), seed]).standard_normal(out[name].shape)
        drawn = base * np.exp(spread * noise) if base else spread * noise
        out[name] = jnp.asarray(drawn.astype(out[name].dtype))
    for name, factor in factors.items():
        out[name] = (out[name] * factor).astype(out[name].dtype)
    return out
```

```python
from contextlib import ExitStack

import numpy as np

import concourse.bass as bass
from concourse import mybir

F32 = mybir.dt.float32
F16 = mybir.dt.float16
BF16 = mybir.dt.bfloat16
I32 = mybir.dt.int32
U32 = mybir.dt.uint32
U8 = mybir.dt.uint8
ALU = mybir.AluOpType
ACT = mybir.ActivationFunctionType
AX = mybir.AxisListType

P = 128
B = 8
S = 256
SB = S // P
D = 128
TILES = B * SB
CHUNK = 512
CT = CHUNK // P
CHUNKS = B * S // CHUNK
H = 16
HG = 4
GROUPS = H // HG
DH0 = 64
DH = D // H
PAIRS = H // 2
E0, F0 = 16, 512
E1, I1 = 8, 64
E2, I2 = 16, 64
EMAX = 16
FT0 = F0 // P
VW = D + H
VLEN = D + H * (VW + 1) + 8
BIG = 1e30
FLOOR = -5e29
EPS = 1e-5
ROUND = 1.5 * 2.0 ** 23


def shape_constants():
    pos = np.arange(S, dtype=np.float64)
    base = (np.arange(0, DH, 2) + 0.4 * DH) / (1.4 * DH)
    scale = base[None, :] ** (pos / 512.0)[:, None]
    freq = 1.0 / 10000.0 ** (np.arange(DH // 2) / (DH // 2))
    angle = pos[:, None] * freq[None, :]
    gamma = 1.0 - np.exp(np.linspace(np.log(1 / 32), np.log(1 / 512), H))
    sign = np.tile([-1.0, 1.0], DH // 2)
    turn = []
    for s, g in ((scale, gamma[None, :] ** pos[:, None]), (1 / scale, gamma[None, :] ** -pos[:, None])):
        for f in (np.cos(angle), np.sin(angle)):
            row = np.repeat(f * s, 2, axis=-1)
            if f[0, 0] == 0.0:
                row = row * sign
            turn.append((g[:, :, None] * row[:, None, :]).reshape(S, D))
    turn = np.stack(turn).reshape(4, SB, P, D).transpose(2, 0, 1, 3)
    p = np.arange(P)
    row = p % 32
    split = np.stack([-(row // 8 == 2).astype(float), -(row // 8 == 1).astype(float)], 1)
    causal = (p[None, :] >= p[:, None]).astype(float)
    own = (p[:, None] // DH == np.arange(H)[None, :]).astype(float)
    block = (p[:, None] // DH == p[None, :] // DH).astype(float)
    expert = (np.arange(EMAX)[:, None, None] == 2 * np.arange(EMAX // 2)[None, :, None] + p[None, None, :] // 64)
    at = np.broadcast_to(np.arange(EMAX, dtype=float), (P, EMAX))
    return {
        "c_eye": np.eye(P), "c_turn": turn, "c_split": split, "c_causal": causal, "c_own": own,
        "c_block": block, "c_expert": expert.astype(float), "c_at": at,
    }


class Chain:

    def __init__(self, eng, sem):
        self.eng, self.sem, self.base, self.n = eng, sem, 0, 0

    def step(self, ins):
        ins.then_inc(self.sem, 1)
        self.n += 1
        return self

    def settle(self):
        self.eng.wait_ge(self.sem, self.base + self.n)

    def turn(self, i, per):
        self.start, self.per = self.base + self.n, per
        self.base, self.n = i * per + self.start, 0

    def turned(self, turns):
        assert self.n == self.per, (self.n, self.per)
        self.base, self.n = self.start + turns * self.per, 0


def wait(eng, sem, value):
    if isinstance(value, int) and value <= 0:
        return
    eng.wait_ge(sem, value)


def wait_alone(eng, sem, value, step):
    eng.wait_ge(sem, value)
    eng.sem_inc(step, 1)


class Seq:

    def __init__(self, i, p):
        self.i, self.p, self.b = i, p, i * 2 + p

    def move(self, n):
        return Seq(self.i + (self.p + n) // 2, (self.p + n) % 2) if n else self


def build(nc, io, out, upto=99):
    ctx = ExitStack()
    with ctx:
        def sem(name):
            return ctx.enter_context(nc.semaphore(name))

        bank = [ctx.enter_context(nc.psum_tensor(f"bank{k}", [P, 512], F32)) for k in range(8)]
        width = 53100
        sbuf = ctx.enter_context(nc.sbuf_tensor("sbuf", [P, width], F32))
        top = [0]

        def take(shape, dt=F32):
            n = int(np.prod(shape))
            words = -(-n * mybir.dt.size(dt) // 32) * 8
            assert top[0] + words <= width, (top[0], words)
            flat = sbuf[:, top[0]:top[0] + words]
            top[0] += words
            flat = (flat if dt == F32 else flat.bitcast(dt))[:, 0:n]
            if len(shape) == 2:
                flat = flat.rearrange("p (a b) -> p a b", b=shape[1])
            if len(shape) == 3:
                flat = flat.rearrange("p (a b c) -> p a b c", b=shape[1], c=shape[2])
            return flat

        x = take([TILES, D])
        xn_t = take([B * S])
        eye = take([P])
        eye16 = take([P], BF16)
        ones = take([P])
        drop = take([P], BF16)
        split = take([2])
        half = take([TILES])
        phases = top[0]

        top[0] = 36800
        far = {}
        for name, shape in (
            ("keys_t", [EMAX]), ("rw_t", [EMAX]), ("rb", [EMAX]), ("b2", [D]), ("at", [EMAX]),
            ("wq1", [HG, P]), ("wk1", [HG, P]), ("wv1", [D]), ("wo1", [D]), ("bq1", [HG]), ("bk1", [HG]),
            ("bv1", [D]), ("bo1", [D]),
            ("gate1", [E1]), ("lb1", [E1]), ("wg1", [5, P]), ("wu1", [5, P]), ("wd1", [5, D]), ("expert", [EMAX // 2, P]),
            ("gate2", [E2]), ("wg2", [10, P]), ("wu2", [2, P]), ("wd2", [10, D]),
            ("wq3", [HG, P]), ("wk3", [HG, P]), ("wv3", [D]), ("wo3", [D]), ("bq3", [HG]), ("bk3", [HG]),
            ("bv3", [D]), ("bo3", [D]),
            ("w_fc", [4, D]), ("w_proj", [F0]), ("u_t", [F0]), ("v", [D]), ("fast_b", [16]), ("gate", [1]),
            ("causal", [P]), ("own", [H]), ("block", [P]), ("turn", [4 * SB * D]),
        ):
            far[name] = take(shape)

        x_in = sem("x_in")
        const_in = sem("const_in")
        far_in = sem("far_in")
        w0_in = sem("w0_in")
        biast_in = [sem(f"biast_in{g}") for g in range(GROUPS)]
        biasq_in = [sem(f"biasq_in{g}") for g in range(GROUPS)]
        eyes_ready = sem("eyes_ready")
        sp_step = sem("sp_step")
        far_loads = [0]
        FAR_LOADS = len(far)

        x_done = sem("x_done")
        x_steps = [0]
        nonlocal_x = [0]

        programs = {"sync": [], "gpsimd": [], "scalar": [], "vector": [], "tensor": []}
        dve_chain = sem("dve_chain")
        chains = {}

        def dve(eng):
            if "v" not in chains:
                chains["v"] = Chain(eng, dve_chain)
            return chains["v"]

        def start_sync(sp):
            sp.dma_start(x, io["x"]).then_inc(x_in, 16)
            sp.dma_start(eye, io["c_eye"]).then_inc(const_in, 16)
            sp.dma_start(split, io["c_split"]).then_inc(const_in, 16)

        def start_vector(v):
            c = dve(v)
            v.memset(ones, 1.0).then_inc(eyes_ready, 1)
            v.memset(drop, -1.0).then_inc(eyes_ready, 1)
            v.wait_ge(const_in, 32)
            v.tensor_copy(eye16, eye).then_inc(eyes_ready, 1)

        programs["sync"].append(start_sync)
        programs["vector"].append(start_vector)

        def far_sync(sp):
            wait(sp, x_done, nonlocal_x[0])
            for name, tile in far.items():
                src = io[name]
                rows = src.shape[0]
                if name in ("rb", "lb1"):
                    src = src.partition_broadcast(P) if len(src.shape) == 1 else src.to_broadcast(list(tile.shape))
                    rows = P
                sp.dma_start(tile[0:rows], src).then_inc(far_in, 16)

        nrm_dve = sem("nrm_stats")
        nrm_rstd = sem("nrm_rstd")
        nrm_xn = sem("nrm_xn")
        nrm_turned = sem("nrm_turned")
        nrm_xt = sem("nrm_xt")
        g_const = sem("g_const")
        g_psum = sem("g_psum")
        g_val = sem("g_val")
        g_exp = sem("g_exp")
        g_ready = sem("g_ready")
        g_turned = sem("g_turned")
        g_t = sem("g_t")
        norms = [0]
        count = {"const": 0, "psum": 0, "val": 0, "exp": 0, "ready": 0, "turned": 0}

        top[0] = phases
        xn = take([TILES, D])
        stats = take([TILES, 6])
        mv = take([TILES, 2])
        var = take([TILES])
        rstd = take([TILES])
        gates = take([TILES, EMAX])
        gates_t = take([B * S])
        logits = take([TILES, EMAX])
        top8 = take([TILES, 8])
        index = take([TILES, 8], U32)
        indexf = take([TILES, 8])
        wk = take([TILES, 8])
        wsum = take([TILES])
        wrec = take([TILES])
        hit = take([TILES, EMAX])
        hitw = take([TILES, EMAX])
        chosen = take([TILES, EMAX])
        sums = take([2 * E1])
        wmean = take([4])
        expert1 = take([E1 // 2, P])
        g0 = take([EMAX])
        g0b = take([EMAX])
        key2 = take([EMAX])
        body = top[0]

        def norm(kind, need_t=True):
            n = norms[0]
            norms[0] += 1
            at_x = x_steps[0]

            def vector(v):
                c = dve(v)
                v.wait_ge(x_in, 16)
                wait(v, x_done, at_x)
                if n == 0:
                    v.memset(half, -0.5).then_inc(nrm_dve, 1)
                for t in range(TILES):
                    last = v.bn_stats(stats[:, t, :], x[:, t, :])
                c.step(last).settle()
                for t in range(TILES):
                    last = v.bn_aggr(mv[:, t, :], stats[:, t, :])
                c.step(last).settle()
                v.tensor_scalar(var, mv[:, :, 1], EPS, None, ALU.add).then_inc(nrm_dve, 1)
                v.wait_ge(nrm_rstd, n + 1)
                for k in range(CHUNKS):
                    for t in range(CT * k, CT * k + CT):
                        last = v.tensor_scalar(xn[:, t, :], x[:, t, :], mv[:, t, 0:1], rstd[:, t:t + 1],
                                               ALU.subtract, ALU.mult)
                    last.then_inc(nrm_xn, 1)

            def pool(g):
                g.wait_ge(nrm_dve, n + 2)
                g.tensor_tensor(rstd, var, half, ALU.pow).then_inc(nrm_rstd, 1)

            def tensor(pe):
                if n == 0:
                    pe.wait_ge(const_in, 32)
                for k in range(CHUNKS):
                    pe.wait_ge(nrm_xn, CHUNKS * n + k + 1)
                    if k >= 2:
                        pe.wait_ge(nrm_xt, CHUNKS * nt + k - 1)
                    for j in range(CT):
                        last = pe.transpose(bank[k % 2][:, j * P:(j + 1) * P], xn[:, CT * k + j, :], eye)
                    last.then_inc(nrm_turned, 1)

            def scalar(act):
                for k in range(CHUNKS):
                    act.wait_ge(nrm_turned, CHUNKS * nt + k + 1)
                    act.activation(xn_t[:, k * CHUNK:(k + 1) * CHUNK], bank[k % 2][:, :], ACT.Copy).then_inc(nrm_xt, 1)

            programs["vector"].append(vector)
            programs["gpsimd"].append(pool)
            if need_t:
                nt = turns[0]
                turns[0] += 1
                programs["tensor"].append(tensor)
                programs["scalar"].append(scalar)

        turns = [0]

        def gate(layer):
            E = (E0, E1, E2)[layer]
            K = (4, 2, 2)[layer]
            at_t = CHUNKS * turns[0]
            base = dict(count)
            weights = (g0, far["gate1"], far["gate2"])[layer]
            count["const"] += layer == 0
            count["psum"] += (2, 2, 1)[layer] + (CHUNKS if layer == 0 else 0)
            count["val"] += 1
            count["exp"] += 1
            count["ready"] += 1 + (layer == 1)
            count["turned"] += CHUNKS
            xb = x_steps[0]
            if layer == 0:
                x_steps[0] += CHUNKS

            def wide(col):
                return col.unsqueeze(2).to_broadcast([P, TILES, E])

            def vector(v):
                c = dve(v)
                if layer == 0:
                    v.wait_ge(far_in, 16 * FAR_LOADS)
                    v.scalar_tensor_tensor(g0, far["keys_t"], 2.0, far["rw_t"], ALU.mult, ALU.add)
                    v.scalar_tensor_tensor(key2, far["keys_t"], -1.0, far["keys_t"], ALU.mult, ALU.mult)\
                     .then_inc(g_const, 1)
                    v.wait_ge(g_psum, base["psum"] + 1)
                    c.step(v.tensor_tensor(g0b, bank[3][:, 0:E], far["rb"], ALU.add)).settle()
                    c.step(v.tensor_tensor(wsum, mv[:, :, 1], rstd, ALU.mult)).settle()
                    c.step(v.tensor_tensor(wsum, wsum, rstd, ALU.mult)).settle()
                L = logits[:, :, 0:E]
                got = bank[2][:, 0:TILES * E].rearrange("p (t e) -> p t e", e=E)
                v.wait_ge(g_psum, base["psum"] + (1 if layer else 2))
                if layer == 0:
                    c.step(v.tensor_tensor(L, got, g0b.unsqueeze(1).to_broadcast([P, TILES, E]), ALU.add)).settle()
                    c.step(v.scalar_tensor_tensor(L, wide(wsum), -float(D), L, ALU.mult, ALU.add)).settle()
                elif layer == 1:
                    c.step(v.tensor_tensor(L, got, far["lb1"].unsqueeze(1).to_broadcast([P, TILES, E]), ALU.add))
                    c.settle()
                    v.tensor_scalar(hit[:, :, 0:E], L, -1.0, None, ALU.mult).then_inc(g_val, 1)
                    v.wait_ge(g_exp, base["exp"] + 1)
                    c.step(v.tensor_scalar(hitw[:, :, 0:E], hitw[:, :, 0:E], 1.0, None, ALU.add)).settle()
                    c.step(v.reciprocal(L, hitw[:, :, 0:E])).settle()
                else:
                    c.step(v.tensor_copy(L, got)).settle()
                for t in range(TILES):
                    last = v.max(top8[:, t, :], logits[:, t, 0:E])
                c.step(last).settle()
                for t in range(TILES):
                    last = v.max_index(index[:, t, :], top8[:, t, :], logits[:, t, 0:E])
                c.step(last).settle()
                c.step(v.tensor_copy(indexf, index)).settle()
                w = wk[:, :, 0:K]
                if layer == 1:
                    c.step(v.tensor_tensor(wsum, top8[:, :, 0], top8[:, :, 1], ALU.add)).settle()
                    c.step(v.tensor_scalar(wsum, wsum, 1e-8, None, ALU.add)).settle()
                    source = top8
                else:
                    v.tensor_tensor(w, top8[:, :, 0:K], top8[:, :, 0:1].to_broadcast([P, TILES, K]), ALU.subtract)\
                     .then_inc(g_val, 1)
                    v.wait_ge(g_exp, base["exp"] + 1)
                    c.step(v.tensor_reduce(wsum, w, AX.X, ALU.add)).settle()
                    source = wk
                c.step(v.reciprocal(wrec, wsum)).settle()
                c.step(v.tensor_tensor(w, source[:, :, 0:K], wrec.unsqueeze(2).to_broadcast([P, TILES, K]), ALU.mult))
                c.settle()
                G, C, Hh, Hw = gates[:, :, 0:E], chosen[:, :, 0:E], hit[:, :, 0:E], hitw[:, :, 0:E]
                slots = far["at"][:, 0:E].unsqueeze(1).to_broadcast([P, TILES, E])
                for k in range(K):
                    first = k == 0
                    Ht = C if first and layer == 1 else Hh
                    c.step(v.tensor_tensor(Ht, slots, wide(indexf[:, :, k]), ALU.is_equal)).settle()
                    c.step(v.tensor_tensor(G if first else Hw, Ht, wide(wk[:, :, k]), ALU.mult)).settle()
                    if not first:
                        c.step(v.tensor_tensor(G, G, Hw, ALU.add)).settle()
                        if layer == 1:
                            c.step(v.tensor_tensor(C, C, Hh, ALU.add)).settle()
                if layer == 1:
                    v.tensor_reduce(sums[:, 0:E], G.rearrange("p t e -> p e t"), AX.X, ALU.add)
                    v.tensor_reduce(sums[:, E:2 * E], C.rearrange("p t e -> p e t"), AX.X, ALU.add).then_inc(g_ready, 2)
                    v.wait_ge(g_psum, base["psum"] + 2)
                    c.step(v.tensor_scalar(wmean[0:E, 0:1], bank[3][0:E, 1:2], 1.0, None, ALU.max)).settle()
                    c.step(v.reciprocal(wmean[0:E, 1:2], wmean[0:E, 0:1])).settle()
                    c.step(v.tensor_tensor(wmean[0:E, 2:3], bank[3][0:E, 0:1], wmean[0:E, 1:2], ALU.mult)).settle()
                    v.tensor_scalar(expert1[0:E], far["expert"][0:E, 0:E // 2, :], wmean[0:E, 2:3], None, ALU.mult)\
                     .then_inc(g_const, 1)
                else:
                    c.settle()
                    c.step(v.tensor_copy(hit[:, :, 0:E], G)).settle()
                    v.tensor_copy(wsum, wsum).then_inc(g_ready, 1)
                if layer == 0:
                    for k in range(CHUNKS):
                        v.wait_ge(g_psum, base["psum"] + 3 + k)
                        xs = x[:, CT * k:CT * k + CT, :]
                        v.tensor_tensor(xs, xs, bank[k][:, :].rearrange("p (t d) -> p t d", d=D), ALU.add)\
                         .then_inc(x_done, 1)

            def scalar(act):
                act.wait_ge(g_val, base["val"] + 1)
                if layer == 1:
                    act.activation(hitw[:, :, 0:E], hit[:, :, 0:E], ACT.Exp).then_inc(g_exp, 1)
                else:
                    act.activation(wk[:, :, 0:K], wk[:, :, 0:K], ACT.Exp).then_inc(g_exp, 1)
                for k in range(CHUNKS):
                    act.wait_ge(g_turned, base["turned"] + k + 1)
                    act.activation(gates_t[0:E, k * CHUNK:(k + 1) * CHUNK], bank[4 + k][0:E, :], ACT.Copy)\
                       .then_inc(g_t, 1)

            def tensor(pe):
                if layer == 0:
                    pe.wait_ge(g_const, base["const"] + 1)
                    pe.matmul(bank[3][:, 0:E], ones, key2, start=True, stop=True).then_inc(g_psum, 1)
                else:
                    pe.wait_ge(far_in, 16 * FAR_LOADS)
                for t in range(TILES):
                    if t % CT == 0:
                        pe.wait_ge(nrm_xt, at_t - CHUNKS + t // CT + 1)
                    last = pe.matmul(bank[2][:, t * E:(t + 1) * E], xn_t[:, t * P:(t + 1) * P], weights[:, 0:E],
                                     start=True, stop=True)
                last.then_inc(g_psum, 1)
                pe.wait_ge(g_ready, base["ready"] + (2 if layer == 1 else 1))
                if layer == 1:
                    pe.matmul(bank[3][0:E, 0:1], sums[:, 0:E], ones[:, 0:1], start=True, stop=True)
                    pe.matmul(bank[3][0:E, 1:2], sums[:, E:2 * E], ones[:, 0:1], start=True, stop=True)\
                      .then_inc(g_psum, 1)
                source = chosen if layer == 1 else gates
                for k in range(CHUNKS):
                    for j in range(CT):
                        last = pe.transpose(bank[4 + k][0:E, j * P:(j + 1) * P], source[:, CT * k + j, 0:E], eye)
                    last.then_inc(g_turned, 1)
                if layer == 0:
                    for k in range(CHUNKS):
                        pe.wait_ge(g_t, base["turned"] + k + 1)
                        for j in range(CT):
                            t = CT * k + j
                            last = pe.matmul(bank[k][:, j * P:(j + 1) * P], gates_t[0:E, t * P:(t + 1) * P],
                                             far["b2"][0:E, :], start=True, stop=True)
                        last.then_inc(g_psum, 1)

            programs["vector"].append(vector)
            programs["scalar"].append(scalar)
            programs["tensor"].append(tensor)
            return base["turned"] + CHUNKS

        def plan(first, last):
            jobs = list(range(12 if not last else 0))
            for g in range(GROUPS):
                for j in range(HG):
                    ahead = (0, g + 1) if g + 1 < GROUPS else (1, 0)
                    if not (last and ahead[0]):
                        yield "scores", *ahead, j
                    yield "weigh", 0, g, j
                    if g or j:
                        yield "mix", 0, *divmod(4 * g + j - 1, 4)
                    elif not first:
                        yield "mix", -1, GROUPS - 1, HG - 1
                    if g == 0 and j == 1 and not first:
                        yield "gather", -1, 0, 0
                    if g == 0 and j == 3 and not first:
                        yield "out", -1, 0, 0
                    if jobs and (g, j) >= (0, 2):
                        if (g, j) == (0, 2):
                            yield "masks", 1, 0, 0
                        yield "project", 1, jobs.pop(0), 0
                if not (last and ahead[0]):
                    yield "maxima", *ahead, 0

        OPEN = [("masks", 0, 0, 0), *[("project", 0, k, 0) for k in range(12)],
                *[("scores", 0, 0, j) for j in range(HG)], ("maxima", 0, 0, 0)]
        CLOSE = [("mix", 0, GROUPS - 1, HG - 1), ("gather", 0, 0, 0), ("out", 0, 0, 0)]

        def walk(eng, steps, chain=None):
            def take_steps(order, at):
                for name, ahead, g, j in order:
                    if name in steps:
                        steps[name](eng, at.move(ahead), g, j)
            take_steps(OPEN, Seq(0, 0))
            take_steps(plan(True, False), Seq(0, 0))
            with eng.Fori(0, B // 2 - 1) as i:
                if chain:
                    chain.turn(i, steps["chained"])
                take_steps(plan(False, False), Seq(i, 1))
                take_steps(plan(False, False), Seq(i + 1, 0))
                if chain:
                    chain.turned(B // 2 - 1)
            take_steps(plan(False, True), Seq(B // 2 - 1, 1))
            take_steps(CLOSE, Seq(B // 2 - 1, 1))

        def attention(layer, need_t):
            wide = layer == 0
            masked = layer < 3
            L = f"a{layer}_"
            s = {k: sem(L + k) for k in (
                "projected",
                "evacuated",
                "halved",
                "scored",
                "maxed",
                "cut",
                "turned",
                "freed",
                "shifts",
                "weighed",
                "biased",
                "probs",
                "mixed",
                "gathered",
                "masks",
                "att_t",
                "vready",
            )}
            ctx_in = [sem(L + f"ctx_in{p}") for p in range(2)]
            mask_in = [sem(L + f"mask_in{p}") for p in range(2)]
            x0 = x_steps[0]
            x_steps[0] += B
            pads = 2

            top[0] = phases if wide else body
            if wide:
                q32 = [take([PAIRS, S]) for _ in range(2)]
                k32 = [take([PAIRS, S]) for _ in range(2)]
            ctx_t = [take([S]) for _ in range(2)]
            kinds = 1 + (layer == 1)
            probs = take([2, 2 * S])
            biased = take([2, 2 * S]) if masked else None
            row_max = take([2, SB, HG])
            parts = take([SB, P], BF16)
            part_of = parts.rearrange("p m (j r) -> p m j r", r=P // HG)
            shift = take([2, S], BF16)
            if wide:
                wq, wk0, wv, wo = take([1024]), take([1024]), take([1024]), take([PAIRS, D])
                bias_t = take([H, 2 * S])
                bias_q = take([H, 2 * S], BF16)
                q16 = [take([PAIRS, S], BF16) for _ in range(2)]
                k16 = [take([PAIRS, S], BF16) for _ in range(2)]
                val = [take([SB, PAIRS, 2 * P]) for _ in range(2)]
                rden = take([S])
                att_t = [take([PAIRS, S]) for _ in range(2)]
                raw = [take([2, 2 * S], U8) for _ in range(2)]
                add_t = [take([2 * S], BF16) for _ in range(2)]
                add_q = [take([2 * S], BF16) for _ in range(2)]
            else:
                wq, wk0, wv, wo = (far[f"w{c}{layer}"] for c in "qkvo")
                bq, bk, bv, bo = (far[f"b{c}{layer}"] for c in "qkvo")
                x32 = take([2, 2 * S])
                high = take([2, 2 * S], F16)
                qs = [take([GROUPS, S], F16) for _ in range(2)]
                ks = [take([GROUPS, S], F16) for _ in range(2)]
                val = [take([SB, VLEN]) for _ in range(2)]
                rden = take([SB, H])
                att = take([SB, D])
                att_t = [take([S])]
                bqs = take([HG])
                if layer == 1:
                    raw_m = take([2, 2 * S], I32)
                    raw_b = take([2, 2 * S])
                    low = take([2 * S])
                    add_t = [take([2 * S]) for _ in range(2)]
                    add_q = [take([2 * S], BF16) for _ in range(2)]
            if not wide:
                assert top[0] <= 36800
            S_BANK, W_BANK, O_BANK, PR, TR = (0, 1), (2, 3), (4, 5), 6, 7
            JOBS = 12 if wide else 5
            per_out = 2 if not wide else 1

            def head(q, g, j):
                return q.b * H + HG * g + j

            def group(q, g):
                return q.b * GROUPS + g

            def tr_job(kind, q, g=0):
                per = GROUPS + per_out
                if kind == "maxima":
                    if isinstance(q.b, int) and q.b == 0:
                        return g
                    if g:
                        return q.b * per + (g - 1) + 1 + GROUPS - per + per_out
                    return q.b * per + 1 + GROUPS - per - 1
                return q.b * per + 1 + GROUPS + kind - (isinstance(q.b, int) and q.b == B - 1)

            def sync(sp):
                if wide:
                    sp.dma_start(ctx_t[0], io["ctx_t"][:, 0:S]).then_inc(ctx_in[0], 16)
                    for tile, name in ((wq, "wq0"), (wk0, "wk0"), (wv, "wv0"), (wo, "wo0")):
                        sp.dma_start(tile, io[name]).then_inc(w0_in, 16)
                else:
                    wait(sp, x_done, x0)

                def masks(i, p):
                    if wide:
                        wait_raw = i * 2 + p - 1
                        for k, name in enumerate(("mask0_t", "mask0_q")):
                            sp.dma_start(raw[p][:, k, :], io[name][bass.ds(i * 2 + p, 1)].rearrange("b p c -> p (b c)"))\
                              .then_inc(mask_in[p], 16)
                    elif layer == 1:
                        if not isinstance(i, int):
                            wait_alone(sp, s["masks"], i * 2 + p, sp_step)
                        elif p:
                            sp.wait_ge(s["masks"], p)
                        for k, name in enumerate(("t", "q")):
                            for tile, kind in ((raw_m, "mask1_"), (raw_b, "bias1_")):
                                sp.dma_start(tile[:, k, :], io[kind + name][bass.ds(i * 2 + p, 1)].rearrange("b p c -> p (b c)"))\
                                  .then_inc(mask_in[p], 16)

                def contexts(i, p):
                    sp.dma_start(ctx_t[p], io["ctx_t"][:, bass.ds((i * 2 + p) * S, S)]).then_inc(ctx_in[p], 16)

                if not wide:
                    contexts(0, 0)
                masks(0, 0)
                contexts(0, 1)
                if wide:
                    for g in range(GROUPS):
                        sp.dma_start(bias_t[:, HG * g:HG * g + HG, :], io["bias0_t"][:, HG * g:HG * g + HG, :])\
                          .then_inc(biast_in[g], 16)
                masks(0, 1)
                with sp.Fori(1, B // 2) as i:
                    for p in range(2):
                        wait_alone(sp, s["projected"], (i * 2 + p - 1) * JOBS, sp_step)
                        contexts(i, p)
                        if wide:
                            wait_alone(sp, s["masks"], i * 2 + p - 1, sp_step)
                        masks(i, p)

            def pool(g):
                if wide:
                    for k in range(GROUPS):
                        g.dma_start(bias_q[:, HG * k:HG * k + HG, :], io["bias0_q"][:, HG * k:HG * k + HG, :])\
                         .then_inc(biasq_in[k], 16)
                else:
                    g.wait_ge(x_done, x0)
                for p in range(2):
                    g.memset(val[p], 1.0 if wide else 0.0).then_inc(s["vready"], 1)
                if not wide:
                    g.wait_ge(s["vready"], 2)
                    for p in range(2):
                        for t in range(SB):
                            g.memset(val[p][:, t, D:D + H * (VW + 1)].rearrange("p (h c) -> p h c", c=VW + 1)[:, :, 0:1],
                                     1.0).then_inc(s["vready"], 1)

            def tensor(pe):
                if wide:
                    pe.wait_ge(eyes_ready, 3)
                    pe.wait_ge(w0_in, 64)
                    pe.wait_ge(nrm_xt, CHUNKS * need_t)
                else:
                    pe.wait_ge(far_in, 16 * FAR_LOADS)
                    pe.wait_ge(nrm_xt, CHUNKS * need_t)

                def project(pe, q, k, _):
                    if k >= JOBS:
                        return
                    wait(pe, s["evacuated"], q.b * JOBS + k)
                    if k == 0:
                        pe.wait_ge(ctx_in[q.p], q.i * 16 + 16)
                    bk_ = bank[PR]
                    xt = xn_t[:, bass.ds(q.b * S, S)]
                    ct = ctx_t[q.p]
                    if k < (8 if wide else 4):
                        kind, pair = divmod(k, 4 if wide else 2)
                        w = (wq, wk0)[kind]
                        for c in range(2):
                            m = 2 * pair + c
                            lhs = w[:, m * P:(m + 1) * P] if wide else w[:, m, :]
                            last = pe.matmul(bk_[:, c * S:(c + 1) * S], lhs, ct if kind else xt, start=True, stop=True)
                    elif wide:
                        t, hf = divmod(k - 8, 2)
                        last = pe.matmul(bk_[:, :], ct[:, t * P:(t + 1) * P], wv[:, hf * 512:(hf + 1) * 512],
                                         start=True, stop=True)
                    else:
                        for t in range(SB):
                            o = bk_[:, t * P:(t + 1) * P]
                            pe.matmul(o, ct[:, t * P:(t + 1) * P], wv, start=True, stop=False)
                            last = pe.matmul(o, ones[0:1, :], bv[0:1, :], start=False, stop=True)
                    last.then_inc(s["projected"], 1)

                def scores(pe, q, g, j):
                    n = head(q, g, j)
                    wait(pe, s["maxed"], n - 1)
                    if g == 0 and j == 0:
                        if wide:
                            wait(pe, s["evacuated"], q.b * JOBS + 8)
                        else:
                            wait(pe, s["halved"], q.b * 4 + 5)
                        if masked:
                            pe.wait_ge(s["masks"], q.b + 1)
                    sc = bank[S_BANK[j % 2]]
                    if wide:
                        if isinstance(q.b, int) and q.b == 0 and j == 0:
                            pe.wait_ge(biasq_in[g], 16)
                        r, t = 64 * (j % 2), 2 * g + j // 2
                        pe.matmul(sc[:, :], eye16, bias_q[:, HG * g + j, :], start=True, stop=False, skip_group_check=True)
                        pe.matmul(sc[:, :], eye16, add_q[q.p], start=False, stop=False, skip_group_check=True)
                        for m in range(SB):
                            last = pe.matmul(sc[:, m * S:(m + 1) * S], q16[q.p][r:r + DH0, t, m * P:(m + 1) * P],
                                             k16[q.p][r:r + DH0, t, :], start=False, stop=m == 1, skip_group_check=True)
                    else:
                        r = 32 * j
                        if masked:
                            pe.matmul(sc[:, :], eye16, add_q[q.p], start=True, stop=False, skip_group_check=True)
                        for m in range(SB):
                            last = pe.matmul(sc[:, m * S:(m + 1) * S], qs[q.p][r:r + 3 * DH, g, m * P:(m + 1) * P],
                                             ks[q.p][r:r + 3 * DH, g, :], start=not masked, stop=True,
                                             skip_group_check=masked)
                    last.then_inc(s["scored"], 1)

                def maxima(pe, q, g, _):
                    pe.wait_ge(s["cut"], group(q, g) * 2 + 2)
                    job = tr_job("maxima", q, g)
                    wait(pe, s["freed"], job)
                    to = bank[TR][:, 0:S // 2].bitcast(BF16)
                    for m in range(SB):
                        last = pe.transpose(to[:, m * P:(m + 1) * P], parts[:, m, :], eye16)
                    last.then_inc(s["turned"], 1)

                def weigh(pe, q, g, j):
                    n = head(q, g, j)
                    wait(pe, s["biased" if masked else "probs"], n - 1)
                    if j == 0:
                        pe.wait_ge(s["shifts"], group(q, g) + 1)
                    o = bank[W_BANK[j % 2]]
                    own = slice(P // HG * j, P // HG * j + 2)
                    sh = shift[own, g % 2, :]
                    if wide:
                        r, t = 64 * (j % 2), 2 * g + j // 2
                        pe.matmul(o[:, :], eye16, add_t[q.p], start=True, stop=False, skip_group_check=True)
                        for m in range(SB):
                            c = o[:, m * S:(m + 1) * S]
                            pe.matmul(c, drop[own, :], sh, start=False, stop=False, skip_group_check=True)
                            last = pe.matmul(c, k32[q.p][r:r + DH0, t, m * P:(m + 1) * P], q32[q.p][r:r + DH0, t, :],
                                             start=False, stop=m == 1, skip_group_check=True)
                    else:
                        r = 32 * j
                        for m in range(SB):
                            c = o[:, m * S:(m + 1) * S]
                            pe.matmul(c, ks[q.p][r:r + 3 * DH, g, m * P:(m + 1) * P], qs[q.p][r:r + 3 * DH, g, :],
                                      start=True, stop=False)
                            last = pe.matmul(c, drop[own, :], sh, start=False, stop=True)
                    last.then_inc(s["weighed"], 1)

                def mix(pe, q, g, j):
                    n = head(q, g, j)
                    pe.wait_ge(s["probs"], n + 1)
                    pr = probs[:, j % 2, :]
                    if wide:
                        h = HG * g + j
                        if h == 0:
                            wait(pe, s["evacuated"], q.b * JOBS + 12)
                        if j % 2 == 0:
                            wait(pe, s["gathered"], q.b * PAIRS + h // 2 - 1)
                        o = bank[O_BANK[(h // 2) % 2]][:, (j % 2) * S:(j % 2 + 1) * S]
                        for t in range(SB):
                            last = pe.matmul(o, val[q.p][:, t, h // 2, (j % 2) * P:(j % 2 + 1) * P],
                                             pr[:, t * S:(t + 1) * S], start=t == 0, stop=t == 1)
                    else:
                        h = HG * g + j
                        if h == 0:
                            wait(pe, s["evacuated"], q.b * JOBS + 5)
                            wait(pe, s["gathered"], q.b - 1)
                        for m in range(SB):
                            for t in range(SB):
                                last = pe.matmul(bank[O_BANK[q.p]][:, m * VW:(m + 1) * VW],
                                                 pr[:, t * S + m * P:t * S + (m + 1) * P],
                                                 val[q.p][:, t, h * VW:(h + 1) * VW],
                                                 start=h == 0 and m == 0 and t == 0, stop=h == H - 1 and t == 1,
                                                 skip_group_check=True)
                    last.then_inc(s["mixed"], 1)

                def out(pe, q, _, __):
                    if not wide:
                        wait(pe, s["freed"], tr_job(0, q))
                        pe.wait_ge(s["gathered"], q.b + 1)
                        for m in range(SB):
                            last = pe.transpose(bank[TR][:, m * P:(m + 1) * P], att[:, m, :], eye)
                        last.then_inc(s["turned"], 1)
                        pe.wait_ge(s["att_t"], q.b + 1)
                        wait(pe, s["freed"], tr_job(1, q))
                    else:
                        wait(pe, s["freed"], tr_job(0, q))
                        pe.wait_ge(s["gathered"], q.b * PAIRS + PAIRS)
                    for m in range(SB):
                        o = bank[TR][:, m * P:(m + 1) * P]
                        if wide:
                            for t in range(PAIRS):
                                last = pe.matmul(o, att_t[q.p][:, t, m * P:(m + 1) * P], wo[:, t, :],
                                                 start=t == 0, stop=t == PAIRS - 1)
                        else:
                            pe.matmul(o, att_t[0][:, m * P:(m + 1) * P], wo, start=True, stop=False)
                            last = pe.matmul(o, ones[0:1, :], bo[0:1, :], start=False, stop=True)
                    last.then_inc(s["turned"], 1)

                walk(pe, {"project": project, "scores": scores, "maxima": maxima, "weigh": weigh, "mix": mix, "out": out})

            def scalar(act):
                if not wide:
                    act.wait_ge(far_in, 16 * FAR_LOADS)
                    act.wait_ge(s["halved"], 1)

                def project(act, q, k, _):
                    if k >= JOBS:
                        return
                    act.wait_ge(s["projected"], q.b * JOBS + k + 1)
                    b_ = bank[PR]
                    if k == 0:
                        wait(act, s["weighed"], q.b * H - H)
                    if wide and k < 8:
                        kind, pair = divmod(k, 4)
                        src = b_[:, :].rearrange("p (c s) -> p c s", s=S)
                        if kind == 0:
                            act.activation(q32[q.p][:, 2 * pair:2 * pair + 2, :], src, ACT.Copy, scale=DH0 ** -0.5)
                            last = act.activation(q16[q.p][:, 2 * pair:2 * pair + 2, :], src, ACT.Copy, scale=DH0 ** -0.5)
                        else:
                            act.activation(k32[q.p][:, 2 * pair:2 * pair + 2, :], src, ACT.Copy)
                            last = act.activation(k16[q.p][:, 2 * pair:2 * pair + 2, :], src, ACT.Copy)
                    elif wide:
                        if k == 8:
                            act.wait_ge(s["vready"], 2)
                            wait(act, s["mixed"], q.b * H - H)
                        t, hf = divmod(k - 8, 2)
                        src = b_[:, :].rearrange("p (n two d) -> p n two d", two=2, d=DH0)
                        act.activation(val[q.p][:, t, HG * hf:HG * hf + HG, 0:DH0], src[:, :, 0, :], ACT.Copy)
                        last = act.activation(val[q.p][:, t, HG * hf:HG * hf + HG, 3 * DH0:4 * DH0], src[:, :, 1, :],
                                              ACT.Copy)
                    elif k < 4:
                        wait(act, s["halved"], q.b * 4 + k - 1 + 1)
                        kind, pair = divmod(k, 2)
                        for c in range(2):
                            m = 2 * pair + c
                            bias = (bqs if kind == 0 else bk)[:, m:m + 1]
                            last = act.activation(x32[:, k % 2, c * S:(c + 1) * S], b_[:, c * S:(c + 1) * S], ACT.Identity,
                                                  bias=bias, scale=DH ** -0.5 if kind == 0 else 1.0)
                    else:
                        act.wait_ge(s["vready"], 6)
                        wait(act, s["mixed"], q.b * H - H)
                        for t in range(SB):
                            last = act.activation(val[q.p][:, t, 0:H * (VW + DH)].rearrange("p (h c) -> p h c", c=VW + DH)[:, :, 0:DH],
                                                  b_[:, t * P:(t + 1) * P].rearrange("p (h d) -> p h d", d=DH), ACT.Copy)
                    last.then_inc(s["evacuated"], 1)

                def maxima(act, q, g, _):
                    act.wait_ge(s["turned"], tr_job("maxima", q, g) + 1)
                    wait(act, s["weighed"], group(q, g) * HG - HG)
                    act.activation(shift[:, g % 2, :], bank[TR][:, 0:S // 2].bitcast(BF16), ACT.Copy)\
                       .then_inc(s["shifts"], 1)
                    act.wait_ge(s["shifts"], group(q, g) + 1)
                    act.sem_inc(s["freed"], 1)

                def weigh(act, q, g, j):
                    n = head(q, g, j)
                    act.wait_ge(s["biased" if masked else "weighed"], n + 1)
                    wait(act, s["mixed"], n - 1)
                    src = biased[:, j % 2, :] if masked else bank[W_BANK[j % 2]][:, :]
                    act.activation(probs[:, j % 2, :], src, ACT.Exp).then_inc(s["probs"], 1)

                def out(act, q, _, __):
                    if wide:
                        return
                    act.wait_ge(s["turned"], tr_job(0, q) + 1)
                    act.activation(att_t[0], bank[TR][:, 0:S], ACT.Copy).then_inc(s["att_t"], 1)
                    act.wait_ge(s["att_t"], q.b + 1)
                    act.sem_inc(s["freed"], 1)

                walk(act, {"project": project, "maxima": maxima, "weigh": weigh, "out": out})

            def vector(v):
                c = dve(v)
                if wide:
                    v.wait_ge(w0_in, 64)
                    c.step(v.memset(parts, 0.0)).settle()
                else:
                    v.wait_ge(far_in, 16 * FAR_LOADS)
                    c.step(v.memset(parts, 0.0)).settle()
                    v.tensor_scalar(bqs, bq, DH ** -0.5, None, ALU.mult).then_inc(s["halved"], 1)

                def masks(v, q, _, __):
                    if not masked:
                        return
                    if wide:
                        v.wait_ge(mask_in[q.p], q.i * 32 + 32)
                        wait(v, s["weighed"], q.b * H - H)
                        v.tensor_scalar(add_t[q.p], raw[q.p][:, 0, :], 0.0, -BIG, ALU.is_equal, ALU.mult)
                        last = v.tensor_scalar(add_q[q.p], raw[q.p][:, 1, :], 0.0, -BIG, ALU.is_equal, ALU.mult)
                    else:
                        v.wait_ge(mask_in[q.p], q.i * 64 + 64)
                        for k, to in enumerate((add_t[q.p], add_q[q.p])):
                            if k == 1:
                                wait(v, s["scored"], q.b * H - H)
                            c.step(v.tensor_scalar(low, raw_m[:, k, :], 0.0, -BIG, ALU.is_equal, ALU.mult)).settle()
                            last = v.tensor_tensor(to, low, raw_b[:, k, :], ALU.add)
                            if k == 0:
                                c.step(last).settle()
                    last.then_inc(s["masks"], 1)

                def project(v, q, k, _):
                    if wide or k >= 4:
                        return
                    v.wait_ge(s["evacuated"], q.b * JOBS + k + 1)
                    kind, pair = divmod(k, 2)
                    c.step(v.tensor_copy(high[:, k % 2, :], x32[:, k % 2, :])).settle()
                    if k == 0:
                        wait(v, s["weighed"], q.b * H - H)
                    v.scalar_tensor_tensor((qs, ks)[kind][q.p][:, 2 * pair:2 * pair + 2, :],
                                           high[:, k % 2, :].rearrange("p (a b) -> p a b", b=S), split[:, kind:kind + 1],
                                           x32[:, k % 2, :].rearrange("p (a b) -> p a b", b=S), ALU.mult, ALU.add)\
                     .then_inc(s["halved"], 1)

                def scores(v, q, g, j):
                    v.wait_ge(s["scored"], head(q, g, j) + 1)
                    v.tensor_reduce(row_max[:, g % 2, :, j], bank[S_BANK[j % 2]][:, :].rearrange("p (m c) -> p m c", c=S),
                                    AX.X, ALU.max).then_inc(s["maxed"], 1)

                def maxima(v, q, g, _):
                    v.wait_ge(s["maxed"], group(q, g) * HG + HG)
                    wait(v, s["turned"], tr_job("maxima", q, g))
                    v.tensor_scalar(part_of[:, :, :, 0], row_max[:, g % 2, :, :], FLOOR, None, ALU.max).then_inc(s["cut"], 1)
                    v.wait_ge(s["cut"], group(q, g) * 2 + 1)
                    v.scalar_tensor_tensor(part_of[:, :, :, 1], row_max[:, g % 2, :, :], FLOOR, part_of[:, :, :, 0],
                                           ALU.max, ALU.subtract).then_inc(s["cut"], 1)

                def weigh(v, q, g, j):
                    if not masked:
                        return
                    n = head(q, g, j)
                    v.wait_ge(s["weighed"], n + 1)
                    wait(v, s["probs"], n - 1)
                    if wide:
                        if isinstance(q.b, int) and q.b == 0 and j == 0:
                            v.wait_ge(biast_in[g], 16)
                        add = bias_t[:, HG * g + j, :]
                    else:
                        add = add_t[q.p]
                    v.tensor_tensor(biased[:, j % 2, :], bank[W_BANK[j % 2]][:, :], add, ALU.add).then_inc(s["biased"], 1)

                def mix(v, q, g, j):
                    if not wide or j % 2 == 0:
                        return
                    pair = 2 * g + j // 2
                    v.wait_ge(s["mixed"], head(q, g, j) + 1)
                    o = bank[O_BANK[pair % 2]]
                    if pair == 0:
                        wait(v, s["freed"], tr_job(0, q.move(-2)) + 1 if not isinstance(q.b, int) or q.b >= 2 else 0)
                    lo, hi = slice(0, 64), slice(64, 128)
                    v.reciprocal(rden[lo], o[hi, 0:S])
                    c.step(v.reciprocal(rden[hi], o[lo, S:2 * S])).settle()
                    v.scalar_tensor_tensor(att_t[q.p][lo, pair, :], rden[lo], BIG, o[lo, 0:S], ALU.min, ALU.mult)
                    v.scalar_tensor_tensor(att_t[q.p][hi, pair, :], rden[hi], BIG, o[hi, S:2 * S], ALU.min, ALU.mult)\
                     .then_inc(s["gathered"], 1)

                def gather(v, q, _, __):
                    if wide:
                        return
                    v.wait_ge(s["mixed"], q.b * H + H)
                    o = bank[O_BANK[q.p]][:, 0:SB * VW].rearrange("p (m c) -> p m c", c=VW)
                    c.step(v.reciprocal(rden, o[:, :, D:VW])).settle()
                    wait(v, s["freed"], tr_job(0, q.move(-1)) + 1 if not isinstance(q.b, int) or q.b >= 1 else 0)
                    for m in range(SB):
                        last = v.tensor_tensor(att[:, m, :].rearrange("p (h d) -> p h d", d=DH),
                                               o[:, m, 0:D].rearrange("p (h d) -> p h d", d=DH),
                                               rden[:, m, :].unsqueeze(2).to_broadcast([P, H, DH]), ALU.mult)
                    last.then_inc(s["gathered"], 1)

                def out(v, q, _, __):
                    k = per_out - 1
                    v.wait_ge(s["turned"], tr_job(k, q) + 1)
                    xs = x[:, bass.ds(q.b * SB, SB), :]
                    v.tensor_tensor(xs, bank[TR][:, 0:S].rearrange("p (t d) -> p t d", d=D), xs, ALU.add)\
                     .then_inc(x_done, 1)
                    v.wait_ge(x_done, q.b + 1 + x0)
                    v.sem_inc(s["freed"], 1)

                steps = {"masks": masks, "project": project, "scores": scores, "maxima": maxima, "weigh": weigh,
                         "mix": mix, "gather": gather, "out": out,
                         "chained": 16 if wide else (2 * (4 + 1) + (2 * 3 if layer == 1 else 0))}
                walk(v, steps, c)

            programs["sync"].append(sync)
            programs["gpsimd"].append(pool)
            programs["tensor"].append(tensor)
            programs["scalar"].append(scalar)
            programs["vector"].append(vector)

        def experts0(gated):
            s = {k: sem("e0_" + k) for k in (
                "up",
                "hidden",
                "down",
                "added",
            )}
            w_in = [sem(f"e0_w_in{p}") for p in range(2)]
            x0 = x_steps[0]
            U = CHUNKS * FT0
            TU = 2 * U
            x_steps[0] += E0 * CHUNKS
            top[0] = body
            w1 = [take([F0]) for _ in range(2)]
            w2 = [take([FT0, D]) for _ in range(2)]
            b1 = [take([FT0]) for _ in range(2)]
            hid = take([4, CHUNK])

            def sync(sp):
                def load(i, p):
                    e = i * 2 + p
                    sp.dma_start(w1[p], io["w1"][bass.ds(e, 1)].rearrange("e p f -> p (e f)")).then_inc(w_in[p], 16)
                    sp.dma_start(w2[p], io["w2"][bass.ds(e, 1)].rearrange("e p t d -> p (e t) d")).then_inc(w_in[p], 16)
                    sp.dma_start(b1[p], io["b1"][bass.ds(e, 1)].rearrange("e p f -> p (e f)")).then_inc(w_in[p], 16)
                wait(sp, x_done, nonlocal_x[0])
                load(0, 0)
                load(0, 1)
                with sp.Fori(1, E0 // 2) as i:
                    for p in range(2):
                        wait_alone(sp, s["down"], i * TU - TU + (p + 1) * U, sp_step)
                        load(i, p)

            def tensor(pe):
                pe.wait_ge(x_done, x0)
                pe.wait_ge(g_t, gated)

                with pe.Fori(0, E0 // 2) as i:
                    def up(u):
                        p, c, f = u // U, u // FT0 % CHUNKS, u % FT0
                        if u % U == 0:
                            pe.wait_ge(w_in[p], i * 48 + 48)
                        if u >= 4:
                            pe.wait_ge(s["hidden"], i * TU + u - 3)
                        pe.matmul(bank[u % 4][:, :], w1[p][:, f * P:(f + 1) * P], xn_t[:, c * CHUNK:(c + 1) * CHUNK],
                                  start=True, stop=True).then_inc(s["up"], 1)

                    def down(u):
                        p, c, f = u // U, u // FT0 % CHUNKS, u % FT0
                        out_no = u // FT0
                        pe.wait_ge(s["hidden"], i * TU + u + 1)
                        if f == 0:
                            pe.wait_ge(s["added"], i * 2 * CHUNKS + max(out_no - 1, 0))
                        for j in range(CT):
                            last = pe.matmul(bank[4 + out_no % 2][:, j * P:(j + 1) * P], hid[:, u % 4, j * P:(j + 1) * P],
                                             w2[p][:, f, :], start=f == 0 and j == 0, stop=f == FT0 - 1,
                                             skip_group_check=True)
                        last.then_inc(s["down"], 1)

                    for u in range(TU + 2):
                        if u < TU:
                            up(u)
                        if u >= 2:
                            down(u - 2)

            def scalar(act):
                with act.Fori(0, E0 // 2) as i:
                    for u in range(TU):
                        if u % U == 0:
                            act.wait_ge(w_in[u // U], i * 48 + 48)
                        act.wait_ge(s["up"], i * TU + u + 1)
                        act.wait_ge(s["down"], i * TU + max(u - 3, 0))
                        act.activation(hid[:, u % 4, :], bank[u % 4][:, :], ACT.Gelu, bias=b1[u // U][:, u % FT0:u % FT0 + 1])\
                           .then_inc(s["hidden"], 1)

            def vector(v):
                v.wait_ge(x_done, x0)
                with v.Fori(0, E0 // 2) as i:
                    for n in range(2 * CHUNKS):
                        p, k = divmod(n, CHUNKS)
                        v.wait_ge(s["down"], i * TU + (n + 1) * FT0)
                        v.wait_ge(x_done, i * 2 * CHUNKS + n + x0)
                        for j in range(CT):
                            t = CT * k + j
                            last = v.scalar_tensor_tensor(x[:, t, :], bank[4 + n % 2][:, j * P:(j + 1) * P],
                                                          gates[:, t, bass.ds(i * 2 + p, 1)], x[:, t, :],
                                                          ALU.mult, ALU.add)
                        last.then_inc(x_done, 1)
                        v.wait_ge(x_done, i * 2 * CHUNKS + n + 1 + x0)
                        v.sem_inc(s["added"], 1)

            programs["sync"].append(sync)
            programs["tensor"].append(tensor)
            programs["scalar"].append(scalar)
            programs["vector"].append(vector)

        def feed_forward(layer, waits):
            s = {k: sem(f"f{layer}_" + k) for k in (
                "inner",
                "acted",
                "hidden",
                "down",
            )}
            x0 = x_steps[0]
            x_steps[0] += CHUNKS
            top[0] = body
            E = (0, E1, E2, 0)[layer]
            routed = E // 2
            NT = (0, 5, 10, 4)[layer]
            K = 5 if layer == 1 else 4
            acted = take([K, CHUNK])
            hid = take([K, CHUNK])
            if layer == 3:
                fc_t = take([F0])
                proj_t = take([4, D])
                fc_e = take([4, D])
                proj_e = take([F0])
                tern = take([F0])
                scale = take([8])
                low = take([F0])
                made = sem("f3_made")
                made_pe = sem("f3_made_pe")
                stored = sem("stored")
                wg, wd = fc_t, proj_t
            else:
                wg, wu, wd = (far[f"w{c}{layer}"] for c in "gud")
                spread = expert1 if layer == 1 else far["expert"]
            def up_of(t):
                return layer == 1 or (layer == 2 and t >= routed)

            def gated(t):
                return t < routed

            def tensor(pe):
                pe.wait_ge(x_done, x0)
                for q, n in waits:
                    pe.wait_ge(q, n)
                if layer == 3:
                    pe.matmul(bank[0][0:16, :], far["fast_b"][0:16, :], far["u_t"][0:16, :], start=True, stop=True)\
                      .then_inc(made_pe, 1)
                    pe.wait_ge(made, 1)
                    pe.matmul(bank[1][:, :], far["v"][0:16, :], low[0:16, :], start=True, stop=True).then_inc(made_pe, 1)
                    pe.wait_ge(made, 3)
                    for t in range(4):
                        pe.transpose(bank[2][:, t * P:(t + 1) * P], fc_e[:, t, :], eye)
                        last = pe.transpose(bank[3][:, t * P:(t + 1) * P], proj_e[:, t * P:(t + 1) * P], eye)
                    last.then_inc(made_pe, 1)
                    pe.wait_ge(made, 5)

                with pe.Fori(0, CHUNKS // 2) as i:
                    def inner(u):
                        p, t = divmod(u, NT)
                        if u >= 2:
                            pe.wait_ge(s["hidden"], i * 2 * NT + u - 1)
                        xt = xn_t[:, bass.ds((i * 2 + p) * CHUNK, CHUNK)]
                        lhs = wg[:, t * P:(t + 1) * P] if layer == 3 else wg[:, t, :]
                        last = pe.matmul(bank[u % 2][:, :], lhs, xt, start=True, stop=True)
                        if up_of(t):
                            last = pe.matmul(bank[2 + u % 2][:, :], wu[:, t - (routed if layer == 2 else 0), :], xt,
                                             start=True, stop=True)
                        if gated(t):
                            last = pe.matmul(bank[4 + u % 2][:, :], spread[0:E, t, :],
                                             gates_t[0:E, bass.ds((i * 2 + p) * CHUNK, CHUNK)], start=True, stop=True)
                        last.then_inc(s["inner"], 1)

                    def down(u):
                        p, t = divmod(u, NT)
                        pe.wait_ge(s["hidden"], i * 2 * NT + u + 1)
                        if t == 0:
                            pe.wait_ge(x_done, i * 2 + x0)
                        for j in range(CT):
                            last = pe.matmul(bank[6 + p][:, j * P:(j + 1) * P], hid[:, u % K, j * P:(j + 1) * P],
                                             wd[:, t, :], start=t == 0 and j == 0, stop=t == NT - 1,
                                             skip_group_check=True)
                        last.then_inc(s["down"], 1)

                    for u in range(2 * NT + 1):
                        if u < 2 * NT:
                            inner(u)
                        if u >= 1:
                            down(u - 1)

            def scalar(act):
                with act.Fori(0, CHUNKS // 2) as i:
                    for u in range(2 * NT):
                        act.wait_ge(s["inner"], i * 2 * NT + u + 1)
                        act.wait_ge(s["hidden"], i * 2 * NT + max(u - K + 1, 0))
                        act.activation(acted[:, u % K, :], bank[u % 2][:, :], ACT.Relu if layer == 3 else ACT.Silu)\
                           .then_inc(s["acted"], 1)

            def vector(v):
                c = dve(v)
                if layer == 3:
                    v.wait_ge(made_pe, 1)
                    v.tensor_copy(low[0:16, :], bank[0][0:16, :]).then_inc(made, 1)
                    for n, (w, to, shape) in enumerate(((far["w_fc"], fc_e, 4), (far["w_proj"], proj_e, 1))):
                        w3 = w if n == 0 else w.unsqueeze(1)
                        size = D if n == 0 else F0
                        t3 = tern.rearrange("p (a b) -> p a b", b=size)
                        to3 = to if n == 0 else to.unsqueeze(1)
                        sc, rc = scale[:, 0:shape], scale[:, 4:4 + shape]
                        wide = [P, shape, size]
                        c.step(v.scalar_tensor_tensor(t3, w3, -1.0, w3, ALU.mult, ALU.max)).settle()
                        c.step(v.tensor_reduce(sc, t3, AX.X, ALU.add)).settle()
                        c.step(v.tensor_scalar(sc, sc, 1.0 / size, 1e-5, ALU.mult, ALU.max)).settle()
                        c.step(v.reciprocal(rc, sc)).settle()
                        c.step(v.tensor_tensor(t3, w3, rc.unsqueeze(2).to_broadcast(wide), ALU.mult)).settle()
                        c.step(v.tensor_scalar(t3, t3, -1.0, 1.0, ALU.max, ALU.min)).settle()
                        c.step(v.tensor_scalar(t3, t3, ROUND, ROUND, ALU.add, ALU.subtract)).settle()
                        c.step(v.tensor_tensor(t3, t3, w3, ALU.subtract)).settle()
                        c.step(v.tensor_tensor(t3, w3, t3, ALU.add)).settle()
                        v.tensor_tensor(to3, t3, sc.unsqueeze(2).to_broadcast(wide), ALU.mult).then_inc(made, 1)
                        v.wait_ge(made, n + 2)
                    v.wait_ge(made_pe, 3)
                    v.wait_ge(made, 3)
                    v.tensor_copy(proj_t, bank[3][:, :].rearrange("p (t d) -> p t d", d=D)).then_inc(made, 1)
                    c.step(v.tensor_copy(tern, bank[2][:, :])).settle()
                    v.scalar_tensor_tensor(fc_t, bank[1][:, :], far["gate"][:, 0:1], tern, ALU.mult, ALU.add)\
                     .then_inc(made, 1)
                with v.Fori(0, CHUNKS // 2) as i:
                    c.turn(i, 2 * (routed if layer == 1 else 0))
                    for u in range(2 * NT):
                        p, t = divmod(u, NT)
                        v.wait_ge(s["acted"], i * 2 * NT + u + 1)
                        v.wait_ge(s["down"], i * 2 * NT + max(u - K + 1, 0))
                        a, h = acted[:, u % K, :], hid[:, u % K, :]
                        if layer == 3:
                            last = v.tensor_tensor(h, a, a, ALU.mult)
                        elif up_of(t) and gated(t):
                            c.step(v.tensor_tensor(h, a, bank[2 + u % 2][:, :], ALU.mult)).settle()
                            last = v.tensor_tensor(h, h, bank[4 + u % 2][:, :], ALU.mult)
                        else:
                            last = v.tensor_tensor(h, a, bank[(4 if gated(t) else 2) + u % 2][:, :], ALU.mult)
                        last.then_inc(s["hidden"], 1)
                        if t == 0 and p == 1:
                            add(v, i, 0)
                    add(v, i, 1)
                    c.turned(CHUNKS // 2)

            def add(v, i, p):
                v.wait_ge(s["down"], i * 2 * NT + (p + 1) * NT)
                xs = x[:, bass.ds((i * 2 + p) * CT, CT), :]
                v.tensor_tensor(xs, bank[6 + p][:, :].rearrange("p (t d) -> p t d", d=D), xs, ALU.add).then_inc(x_done, 1)

            def sync(sp):
                with sp.Fori(0, CHUNKS) as i:
                    wait_alone(sp, x_done, i + 1 + x0, sp_step)
                    sp.dma_start(out[:, bass.ds(i * CT, CT), :], x[:, bass.ds(i * CT, CT), :]).then_inc(stored, 16)
                sp.wait_ge(stored, 16 * CHUNKS)

            programs["tensor"].append(tensor)
            programs["scalar"].append(scalar)
            programs["vector"].append(vector)
            if layer == 3:
                programs["sync"].append(sync)

        def retention():
            s = {k: sem("r_" + k) for k in (
                "rotated",
                "turned",
                "spread",
                "scored",
                "masked",
                "mixed",
                "state",
                "kept",
                "output",
                "ready",
            )}
            c_in = [sem(f"r_c_in{p}") for p in range(2)]
            x0 = x_steps[0]
            x_steps[0] += B
            normed = CHUNKS * norms[0]
            top[0] = body
            tok = [take([SB, D]) for _ in range(2)]
            qk = [take([2, SB, D]) for _ in range(2)]
            turn_a = take([2, SB, D])
            turn_b = take([2, SB, D])
            k_t = [take([S]) for _ in range(2)]
            q_t = [take([S]) for _ in range(2)]
            q_own = [take([H, S]) for _ in range(2)]
            v_own = [take([SB, H * D + 8 * H]) for _ in range(2)]
            prob = take([3, HG, P])
            kept = take([P])
            assert top[0] <= 36800
            turn = far["turn"].rearrange("p (k t d) -> p k t d", k=4, d=D)
            UNITS = SB * GROUPS

            def plan_r(first, last):
                for u in range(UNITS):
                    yield "scores", 0, u
                    if u >= 1:
                        yield "mix", 0, u - 1
                    if u == 1 and not last:
                        yield "rotate", 1, 0
                    if u == 2:
                        yield "state", 0, 0
                    if u == 4 and not last:
                        yield "turn", 1, 0
                    if u == 1 and not first:
                        yield "add", -1, 0
                yield "mix", 0, UNITS - 1
                yield "inter", 0, 0

            def walk_r(eng, steps, chain=None):
                def go(order, at):
                    for name, ahead, u in order:
                        if name in steps:
                            steps[name](eng, at.move(ahead), u)
                go([("rotate", 0, 0), ("turn", 0, 0)], Seq(0, 0))
                go(plan_r(True, False), Seq(0, 0))
                with eng.Fori(0, B // 2 - 1) as i:
                    if chain:
                        chain.turn(i, steps["chained"])
                    go(plan_r(False, False), Seq(i, 1))
                    go(plan_r(False, False), Seq(i + 1, 0))
                    if chain:
                        chain.turned(B // 2 - 1)
                go(plan_r(False, True), Seq(B // 2 - 1, 1))
                go([("add", 0, 0)], Seq(B // 2 - 1, 1))

            def sync(sp):
                wait(sp, x_done, x0)

                def load(i, p):
                    sp.dma_start(tok[p], io["ctx"][:, bass.ds((i * 2 + p) * SB, SB), :]).then_inc(c_in[p], 16)
                load(0, 0)
                load(0, 1)
                with sp.Fori(1, B // 2) as i:
                    for p in range(2):
                        wait_alone(sp, s["state"], i * 2 + p - 1, sp_step)
                        wait_alone(sp, s["spread"], i * 2 + p - 1, sp_step)
                        load(i, p)

            def pool(g):
                g.wait_ge(x_done, x0)
                for p in range(2):
                    g.memset(v_own[p], 0.0).then_inc(s["ready"], 1)

            def tensor(pe):
                def turn_pe(pe, q, _):
                    pe.wait_ge(s["rotated"], q.b + 1)
                    wait(pe, s["spread"], q.b)
                    for k in range(2):
                        for t in range(SB):
                            last = pe.transpose(bank[2][:, k * S + t * P:k * S + (t + 1) * P], qk[q.p][:, k, t, :], eye)
                    last.then_inc(s["turned"], 1)

                def scores(pe, q, u):
                    t, g = divmod(u, GROUPS)
                    if u == 0:
                        pe.wait_ge(s["spread"], q.b + 1)
                    wait(pe, s["masked"], q.b * UNITS + u - 1)
                    pe.matmul(bank[u % 2][:, :], k_t[q.p][:, t * P:(t + 1) * P],
                              q_own[q.p][:, HG * g:HG * g + HG, t * P:(t + 1) * P], start=True, stop=True)\
                      .then_inc(s["scored"], 1)

                def mix(pe, q, u):
                    t, g = divmod(u, GROUPS)
                    pe.wait_ge(s["masked"], q.b * UNITS + u + 1)
                    if u == 0:
                        wait(pe, x_done, q.b - 1 + x0)
                    for j in range(HG):
                        h = HG * g + j
                        last = pe.matmul(bank[4 + q.p][:, t * P:(t + 1) * P], prob[:, u % 3, j, :],
                                         v_own[q.p][:, t, h * D:(h + 1) * D], start=u == 0 and j == 0,
                                         stop=g == GROUPS - 1 and j == HG - 1 and t == 0, skip_group_check=True)
                    last.then_inc(s["mixed"], 1)

                def state(pe, q, _):
                    pe.wait_ge(s["rotated"], q.b + 1)
                    wait(pe, s["kept"], q.b)
                    pe.matmul(bank[3][:, 0:P], qk[q.p][:, 1, 0, :], tok[q.p][:, 0, :], start=True, stop=True)\
                      .then_inc(s["state"], 1)

                def inter(pe, q, _):
                    pe.wait_ge(s["kept"], q.b + 1)
                    pe.matmul(bank[4 + q.p][:, P:2 * P], q_t[q.p][:, P:2 * P], kept, start=False, stop=True,
                              skip_group_check=True).then_inc(s["output"], 1)

                walk_r(pe, {"turn": turn_pe, "scores": scores, "mix": mix, "state": state, "inter": inter})

            def scalar(act):
                act.wait_ge(far_in, 16 * FAR_LOADS)
                act.wait_ge(s["ready"], 2)

                def turn_act(act, q, _):
                    act.wait_ge(s["turned"], q.b + 1)
                    wait(act, s["output"], q.b - 1)
                    act.activation(k_t[q.p], bank[2][:, S:2 * S], ACT.Copy)
                    act.activation(q_t[q.p], bank[2][:, 0:S], ACT.Copy)
                    for t in range(SB):
                        act.activation(v_own[q.p][:, t, 0:H * (D + DH)].rearrange("p (h c) -> p h c", c=D + DH)[:, :, 0:DH],
                                       tok[q.p][:, t, :].rearrange("p (h d) -> p h d", d=DH), ACT.Copy)
                    for h in range(H):
                        last = act.activation(q_own[q.p][:, h, :], bank[2][:, 0:S], ACT.Copy, scale=far["own"][:, h:h + 1])
                    last.then_inc(s["spread"], 1)

                walk_r(act, {"turn": turn_act})

            def vector(v):
                c = dve(v)
                v.wait_ge(far_in, 16 * FAR_LOADS)
                v.wait_ge(nrm_xn, normed)

                def rotate(v, q, _):
                    v.wait_ge(c_in[q.p], q.i * 16 + 16)
                    wait(v, s["state"], q.b - 1)
                    for k in range(2):
                        src = tok[q.p] if k else xn[:, bass.ds(q.b * SB, SB), :]
                        pair = src.rearrange("p t (n two) -> p t n two", two=2)
                        ta, tb = turn_a[:, k], turn_b[:, k].rearrange("p t (n two) -> p t n two", two=2)
                        sn = turn[:, 2 * k + 1].rearrange("p t (n two) -> p t n two", two=2)
                        v.tensor_tensor(ta, src, turn[:, 2 * k], ALU.mult)
                        v.tensor_tensor(tb[:, :, :, 0], pair[:, :, :, 1], sn[:, :, :, 0], ALU.mult)
                        c.step(v.tensor_tensor(tb[:, :, :, 1], pair[:, :, :, 0], sn[:, :, :, 1], ALU.mult)).settle()
                        last = v.tensor_tensor(qk[q.p][:, k], ta, turn_b[:, k], ALU.add)
                    last.then_inc(s["rotated"], 1)

                def scores(v, q, u):
                    v.wait_ge(s["scored"], q.b * UNITS + u + 1)
                    wait(v, s["mixed"], q.b * UNITS + u - 2)
                    v.tensor_tensor(prob[:, u % 3], bank[u % 2][:, :].rearrange("p (h c) -> p h c", c=P),
                                    far["causal"].unsqueeze(1).to_broadcast([P, HG, P]), ALU.mult).then_inc(s["masked"], 1)

                def state(v, q, _):
                    v.wait_ge(s["state"], q.b + 1)
                    wait(v, s["output"], q.b)
                    v.tensor_tensor(kept, bank[3][:, 0:P], far["block"], ALU.mult).then_inc(s["kept"], 1)

                def add(v, q, _):
                    v.wait_ge(s["output"], q.b + 1)
                    xs = x[:, bass.ds(q.b * SB, SB), :]
                    v.tensor_tensor(xs, bank[4 + q.p][:, 0:S].rearrange("p (t d) -> p t d", d=D), xs, ALU.add)\
                     .then_inc(x_done, 1)

                walk_r(v, {"rotate": rotate, "scores": scores, "state": state, "add": add, "chained": 4}, c)

            programs["sync"].append(sync)
            programs["gpsimd"].append(pool)
            programs["tensor"].append(tensor)
            programs["scalar"].append(scalar)
            programs["vector"].append(vector)

        def sublayers():
            norm(0)
            attention(0, turns[0])
            yield
            nonlocal_x[0] = x_steps[0]
            programs["sync"].append(far_sync)
            norm(1)
            experts0(gate(0))
            yield
            norm(2)
            attention(1, turns[0])
            yield
            norm(3)
            feed_forward(1, [(g_t, gate(1)), (g_const, 2)])
            yield
            norm(4, need_t=False)
            retention()
            yield
            norm(5)
            feed_forward(2, [(g_t, gate(2))])
            yield
            norm(6)
            attention(3, turns[0])
            yield
            norm(7)
            feed_forward(3, [(nrm_xt, CHUNKS * turns[0])])
            yield

        for n, _ in enumerate(sublayers()):
            if n + 1 == upto:
                break

        block = ctx.enter_context(nc.Block())

        @block.sync
        def _(sp):
            for part in programs["sync"]:
                part(sp)

        @block.gpsimd
        def _(g):
            for part in programs["gpsimd"]:
                part(g)

        @block.scalar
        def _(act):
            for part in programs["scalar"]:
                part(act)

        @block.vector
        def _(v):
            for part in programs["vector"]:
                part(v)

        @block.tensor
        def _(pe):
            for part in programs["tensor"]:
                part(pe)


def laid_out(a):
    f = {k: np.ascontiguousarray(v) for k, v in a.items()}
    r = {}
    r["x"] = f["x"].reshape(TILES, P, D).transpose(1, 0, 2)
    r["ctx_t"] = f["ctx_1024"].reshape(B * S, D).T
    r["ctx"] = f["ctx_1024"].reshape(TILES, P, D).transpose(1, 0, 2)
    r["mask0_q"] = f["mask_BxSxS2_bk0"]
    r["mask0_t"] = f["mask_BxSxS2_bk0"].transpose(0, 2, 1)
    r["mask1_q"] = f["mask_Bx1xSxS2_ik1"][:, 0]
    r["mask1_t"] = r["mask1_q"].transpose(0, 2, 1)
    r["bias1_q"] = f["fside_BxSxS2_0"]
    r["bias1_t"] = r["bias1_q"].transpose(0, 2, 1)
    r["bias0_q"] = f["L0_xattn_position_bias"]
    r["bias0_t"] = r["bias0_q"].transpose(0, 2, 1)
    for n in ("mask0_q", "mask0_t", "mask1_q", "mask1_t", "bias1_q", "bias1_t"):
        r[n] = r[n].reshape(B, SB, P, S).transpose(0, 2, 1, 3).reshape(B, P, SB * S)
    for n in ("bias0_q", "bias0_t"):
        r[n] = r[n].reshape(H, SB, P, S).transpose(2, 0, 1, 3).reshape(P, H, SB * S)
    for n, c in (("wq0", "q"), ("wk0", "k"), ("wv0", "v")):
        r[n] = f[f"L0_xattn_W{c}"].T
    r["wo0"] = f["L0_xattn_Wo"].T.reshape(PAIRS, P, D).transpose(1, 0, 2)
    r["keys_t"], r["rw_t"] = f["L0_ffn_keys"].T, f["L0_ffn_rw"].T
    r["rb"], r["b2"] = f["L0_ffn_rb"][None], f["L0_ffn_b2"]
    r["w1"] = f["L0_ffn_w1"].transpose(0, 2, 1)
    r["b1"] = f["L0_ffn_b1"].reshape(E0, FT0, P).transpose(0, 2, 1)
    r["w2"] = f["L0_ffn_w2"].transpose(0, 2, 1).reshape(E0, FT0, P, D).transpose(0, 2, 1, 3)
    rows = (HG * np.arange(GROUPS)[:, None, None] + np.arange(HG)[None, :, None]) * DH + np.arange(32)[None, None] % DH
    rows = rows.reshape(GROUPS, P)
    for n in (1, 3):
        for c in "qk":
            r[f"w{c}{n}"] = f[f"L{n}_xattn_W{c}"].T[:, rows]
            r[f"b{c}{n}"] = f[f"L{n}_xattn_b{c}"][rows].T
        for c in "vo":
            r[f"w{c}{n}"] = f[f"L{n}_xattn_W{c}"].T
            r[f"b{c}{n}"] = f[f"L{n}_xattn_b{c}"][None]
    r["gate1"], r["lb1"] = f["L1_ffn_gate_w"].T, f["L1_ffn_lb_bias"][None]
    for n, c in (("wg1", "gate"), ("wu1", "up")):
        w = np.concatenate([f[f"L1_ffn_expert_{c}_w"].reshape(E1 // 2, P, D), f[f"L1_ffn_shared_{c}_w"][None]])
        r[n] = w.transpose(2, 0, 1)
    w = np.concatenate([f["L1_ffn_expert_down_w"].transpose(0, 2, 1).reshape(E1 // 2, P, D),
                        f["L1_ffn_shared_down_w"].T[None]])
    r["wd1"] = w.transpose(1, 0, 2)
    r["gate2"] = f["L2_ffn_gate_w"].T
    w = np.concatenate([f["L2_ffn_w1"].reshape(E2 // 2, P, D), f["L2_ffn_sfc1"].reshape(2, P, D)])
    r["wg2"] = w.transpose(2, 0, 1)
    r["wu2"] = f["L2_ffn_sfc2"].reshape(2, P, D).transpose(2, 0, 1)
    w = np.concatenate([f["L2_ffn_w2"].transpose(0, 2, 1).reshape(E2 // 2, P, D), f["L2_ffn_sfc3"].T.reshape(2, P, D)])
    r["wd2"] = w.transpose(1, 0, 2)
    r["w_fc"] = f["L3_ffn_w_fc"].reshape(4, P, D).transpose(1, 0, 2)
    r["w_proj"] = f["L3_ffn_w_proj"]
    r["u_t"], r["v"], r["fast_b"] = f["L3_ffn_u"].T, f["L3_ffn_v"], f["L3_ffn_fast_b"]
    r["gate"] = np.broadcast_to(f["L3_ffn_gate"].reshape(1, 1), (P, 1))
    for n, c in shape_constants().items():
        r[n] = c.astype(np.float32)
    for n in ("at", "expert", "causal", "own", "block", "turn"):
        r[n] = r.pop("c_" + n)
    r["turn"] = r["turn"].reshape(P, -1)
    return {n: np.ascontiguousarray(v) for n, v in r.items()}


def kernel(**inputs):
    import concourse.bacc as bacc
    from concourse.bass_utils import run_bass_kernel_spmd

    arrays = laid_out({k: np.asarray(v) for k, v in inputs.items()})
    nc = bacc.Bacc("TRN2", target_bir_lowering=False, num_devices=1)
    io = {n: nc.dram_tensor(n, a.shape, mybir.dt.from_np(a.dtype), kind="ExternalInput").ap()
          for n, a in arrays.items()}
    out = nc.dram_tensor("out", (P, TILES, D), F32, kind="ExternalOutput").ap()
    build(nc, io, out)
    r = run_bass_kernel_spmd(nc, [arrays], core_ids=[0])
    return np.ascontiguousarray(r.results[0]["out"].transpose(1, 0, 2).reshape(B, S, D))
```

```python
from contextlib import ExitStack

import numpy as np

import concourse.bass as bass
from concourse import mybir

F32 = mybir.dt.float32
F16 = mybir.dt.float16
BF16 = mybir.dt.bfloat16
I32 = mybir.dt.int32
U32 = mybir.dt.uint32
U8 = mybir.dt.uint8
ALU = mybir.AluOpType
ACT = mybir.ActivationFunctionType
AX = mybir.AxisListType

P = 128
B = 8
S = 256
SB = S // P
D = 128
TILES = B * SB
CHUNK = 512
CT = CHUNK // P
CHUNKS = B * S // CHUNK
H = 16
HG = 4
GROUPS = H // HG
DH0 = 64
DH = D // H
PAIRS = H // 2
E0, F0 = 16, 512
E1, I1 = 8, 64
E2, I2 = 16, 64
EMAX = 16
FT0 = F0 // P
BIG = 1e30
FLOOR = -5e29
LIFT = 10 * float(np.log(2.0))
EPS = 1e-5
ROUND = 1.5 * 2.0 ** 23


def shape_constants():
    pos = np.arange(S, dtype=np.float64)
    base = (np.arange(0, DH, 2) + 0.4 * DH) / (1.4 * DH)
    scale = base[None, :] ** (pos / 512.0)[:, None]
    freq = 1.0 / 10000.0 ** (np.arange(DH // 2) / (DH // 2))
    angle = pos[:, None] * freq[None, :]
    gamma = 1.0 - np.exp(np.linspace(np.log(1 / 32), np.log(1 / 512), H))
    sign = np.tile([-1.0, 1.0], DH // 2)
    turn = []
    for s, g in ((scale, gamma[None, :] ** pos[:, None]), (1 / scale, gamma[None, :] ** -pos[:, None])):
        for f in (np.cos(angle), np.sin(angle)):
            row = np.repeat(f * s, 2, axis=-1)
            if f[0, 0] == 0.0:
                row = row * sign
            turn.append((g[:, :, None] * row[:, None, :]).reshape(S, D))
    turn = np.stack(turn).reshape(4, SB, P, D).transpose(2, 0, 1, 3)
    p = np.arange(P)
    row = p % 32
    split = np.stack([-(row // 8 >= 2).astype(float), -(row // 8 % 2 == 1).astype(float)], 1)
    causal = (p[None, :] >= p[:, None]).astype(float)
    own = (p[:, None] // DH == np.arange(H)[None, :]).astype(float)
    block = (p[:, None] // DH == p[None, :] // DH).astype(float)
    expert = (np.arange(EMAX)[:, None, None] == 2 * np.arange(EMAX // 2)[None, :, None] + p[None, None, :] // 64)
    drop = -(p[:, None] // 2 == np.arange(HG)[None, :] * (P // HG // 2)).astype(float)
    drop = np.broadcast_to(drop[:, :, None], (P, HG, P))
    at = np.broadcast_to(np.arange(EMAX, dtype=float), (P, EMAX))
    return {
        "c_eye": np.eye(P), "c_turn": turn, "c_split": split, "c_causal": causal, "c_own": own,
        "c_block": block, "c_expert": expert.astype(float), "c_at": at,
        "c_drop": drop,
    }


class Chain:

    def __init__(self, eng, sem):
        self.eng, self.sem, self.base, self.n = eng, sem, 0, 0

    def step(self, ins):
        ins.then_inc(self.sem, 1)
        self.n += 1
        return self

    def settle(self):
        self.eng.wait_ge(self.sem, self.base + self.n)

    def turn(self, i, per):
        self.start, self.per = self.base + self.n, per
        self.base, self.n = i * per + self.start, 0

    def turned(self, turns):
        assert self.n == self.per, (self.n, self.per)
        self.base, self.n = self.start + turns * self.per, 0


def wait(eng, sem, value):
    if isinstance(value, int) and value <= 0:
        return
    eng.wait_ge(sem, value)


def wait_alone(eng, sem, value, step):
    eng.wait_ge(sem, value)
    eng.sem_inc(step, 1)


class Seq:

    def __init__(self, i, p):
        self.i, self.p, self.b = i, p, i * 2 + p

    def move(self, n):
        return Seq(self.i + (self.p + n) // 2, (self.p + n) % 2) if n else self


def build(nc, io, out, upto=99):
    ctx = ExitStack()
    with ctx:
        def sem(name):
            return ctx.enter_context(nc.semaphore(name))

        bank = [ctx.enter_context(nc.psum_tensor(f"bank{k}", [P, 512], F32)) for k in range(8)]
        width = 53100
        sbuf = ctx.enter_context(nc.sbuf_tensor("sbuf", [P, width], F32))
        top = [0]

        def take(shape, dt=F32):
            n = int(np.prod(shape))
            words = -(-n * mybir.dt.size(dt) // 32) * 8
            assert top[0] + words <= width, (top[0], words)
            flat = sbuf[:, top[0]:top[0] + words]
            top[0] += words
            flat = (flat if dt == F32 else flat.bitcast(dt))[:, 0:n]
            if len(shape) == 2:
                flat = flat.rearrange("p (a b) -> p a b", b=shape[1])
            if len(shape) == 3:
                flat = flat.rearrange("p (a b c) -> p a b c", b=shape[1], c=shape[2])
            return flat

        x = take([TILES, D])
        xn_t = take([B * S])
        eye = take([P])
        eye16 = take([P], BF16)
        ones = take([P])
        drop = take([HG, P], BF16)
        split = take([2])
        half = take([TILES])
        phases = top[0]
        drop32 = take([HG, P])

        top[0] = 36800
        far = {}
        for name, shape in (
            ("keys_t", [EMAX]), ("rw_t", [EMAX]), ("rb", [EMAX]), ("b2", [D]), ("at", [EMAX]),
            ("wq1", [HG, P]), ("wk1", [HG, P]), ("wv1", [D]), ("wo1", [D]), ("bq1", [HG]), ("bk1", [HG]),
            ("bv1", [D]), ("bo1", [D]),
            ("gate1", [E1]), ("lb1", [E1]), ("wg1", [5, P]), ("wu1", [5, P]), ("wd1", [5, D]), ("expert", [EMAX // 2, P]),
            ("gate2", [E2]), ("wg2", [10, P]), ("wu2", [2, P]), ("wd2", [10, D]),
            ("wq3", [HG, P]), ("wk3", [HG, P]), ("wv3", [D]), ("wo3", [D]), ("bq3", [HG]), ("bk3", [HG]),
            ("bv3", [D]), ("bo3", [D]),
            ("w_fc", [4, D]), ("w_proj", [F0]), ("u_t", [F0]), ("v", [D]), ("fast_b", [16]), ("gate", [1]),
            ("causal", [P]), ("own", [H]), ("block", [P]), ("turn", [4 * SB * D]),
        ):
            far[name] = take(shape)

        x_in = sem("x_in")
        const_in = sem("const_in")
        far_in = sem("far_in")
        w0_in = sem("w0_in")
        biast_in = [sem(f"biast_in{g}") for g in range(GROUPS)]
        biasq_in = [sem(f"biasq_in{g}") for g in range(GROUPS)]
        eyes_ready = sem("eyes_ready")
        sp_step = sem("sp_step")
        far_loads = [0]
        FAR_LOADS = len(far)

        x_done = sem("x_done")
        x_steps = [0]
        nonlocal_x = [0]

        programs = {"sync": [], "gpsimd": [], "scalar": [], "vector": [], "tensor": []}
        dve_chain = sem("dve_chain")
        chains = {}

        def dve(eng):
            if "v" not in chains:
                chains["v"] = Chain(eng, dve_chain)
            return chains["v"]

        def start_sync(sp):
            sp.dma_start(x, io["x"]).then_inc(x_in, 16)
            sp.dma_start(eye, io["c_eye"]).then_inc(const_in, 16)
            sp.dma_start(split, io["c_split"]).then_inc(const_in, 16)
            sp.dma_start(drop32, io["c_drop"]).then_inc(const_in, 16)

        def start_vector(v):
            c = dve(v)
            v.memset(ones, 1.0).then_inc(eyes_ready, 1)
            v.wait_ge(const_in, 48)
            v.tensor_copy(drop, drop32).then_inc(eyes_ready, 1)
            v.tensor_copy(eye16, eye).then_inc(eyes_ready, 1)

        programs["sync"].append(start_sync)
        programs["vector"].append(start_vector)

        def far_sync(sp):
            wait(sp, x_done, nonlocal_x[0])
            for name, tile in far.items():
                src = io[name]
                rows = src.shape[0]
                if name in ("rb", "lb1"):
                    src = src.partition_broadcast(P) if len(src.shape) == 1 else src.to_broadcast(list(tile.shape))
                    rows = P
                sp.dma_start(tile[0:rows], src).then_inc(far_in, 16)

        nrm_dve = sem("nrm_stats")
        nrm_rstd = sem("nrm_rstd")
        nrm_xn = sem("nrm_xn")
        nrm_turned = sem("nrm_turned")
        nrm_xt = sem("nrm_xt")
        g_const = sem("g_const")
        g_psum = sem("g_psum")
        g_val = sem("g_val")
        g_exp = sem("g_exp")
        g_ready = sem("g_ready")
        g_turned = sem("g_turned")
        g_t = sem("g_t")
        norms = [0]
        count = {"const": 0, "psum": 0, "val": 0, "exp": 0, "ready": 0, "turned": 0}

        top[0] = phases
        xn = take([TILES, D])
        stats = take([TILES, 6])
        mv = take([TILES, 2])
        var = take([TILES])
        rstd = take([TILES])
        gates = take([TILES, EMAX])
        gates_t = take([B * S])
        logits = take([TILES, EMAX])
        top8 = take([TILES, 8])
        index = take([TILES, 8], U32)
        indexf = take([TILES, 8])
        wk = take([TILES, 8])
        wsum = take([TILES])
        wrec = take([TILES])
        hit = take([TILES, EMAX])
        hitw = take([TILES, EMAX])
        chosen = take([TILES, EMAX])
        sums = take([2 * E1])
        wmean = take([4])
        expert1 = take([E1 // 2, P])
        g0 = take([EMAX])
        g0b = take([EMAX])
        key2 = take([EMAX])
        body = top[0]

        def norm(kind, need_t=True):
            n = norms[0]
            norms[0] += 1
            at_x = x_steps[0]

            def vector(v):
                c = dve(v)
                v.wait_ge(x_in, 16)
                wait(v, x_done, at_x)
                if n == 0:
                    v.memset(half, -0.5).then_inc(nrm_dve, 1)
                for t in range(TILES):
                    last = v.bn_stats(stats[:, t, :], x[:, t, :])
                c.step(last).settle()
                for t in range(TILES):
                    last = v.bn_aggr(mv[:, t, :], stats[:, t, :])
                c.step(last).settle()
                v.tensor_scalar(var, mv[:, :, 1], EPS, None, ALU.add).then_inc(nrm_dve, 1)
                v.wait_ge(nrm_rstd, n + 1)
                for k in range(CHUNKS):
                    for t in range(CT * k, CT * k + CT):
                        last = v.tensor_scalar(xn[:, t, :], x[:, t, :], mv[:, t, 0:1], rstd[:, t:t + 1],
                                               ALU.subtract, ALU.mult)
                    last.then_inc(nrm_xn, 1)

            def pool(g):
                g.wait_ge(nrm_dve, n + 2)
                g.tensor_tensor(rstd, var, half, ALU.pow).then_inc(nrm_rstd, 1)

            def tensor(pe):
                if n == 0:
                    pe.wait_ge(const_in, 48)
                for k in range(CHUNKS):
                    pe.wait_ge(nrm_xn, CHUNKS * n + k + 1)
                    if k >= 2:
                        pe.wait_ge(nrm_xt, CHUNKS * nt + k - 1)
                    for j in range(CT):
                        last = pe.transpose(bank[k % 2][:, j * P:(j + 1) * P], xn[:, CT * k + j, :], eye)
                    last.then_inc(nrm_turned, 1)

            def scalar(act):
                for k in range(CHUNKS):
                    act.wait_ge(nrm_turned, CHUNKS * nt + k + 1)
                    act.activation(xn_t[:, k * CHUNK:(k + 1) * CHUNK], bank[k % 2][:, :], ACT.Copy).then_inc(nrm_xt, 1)

            programs["vector"].append(vector)
            programs["gpsimd"].append(pool)
            if need_t:
                nt = turns[0]
                turns[0] += 1
                programs["tensor"].append(tensor)
                programs["scalar"].append(scalar)

        turns = [0]

        def gate(layer):
            E = (E0, E1, E2)[layer]
            K = (4, 2, 2)[layer]
            at_t = CHUNKS * turns[0]
            base = dict(count)
            weights = (g0, far["gate1"], far["gate2"])[layer]
            count["const"] += layer == 0
            count["psum"] += (2, 2, 1)[layer] + (CHUNKS if layer == 0 else 0)
            count["val"] += 1
            count["exp"] += 1
            count["ready"] += 1 + (layer == 1)
            count["turned"] += CHUNKS
            xb = x_steps[0]
            if layer == 0:
                x_steps[0] += CHUNKS

            def wide(col):
                return col.unsqueeze(2).to_broadcast([P, TILES, E])

            def vector(v):
                c = dve(v)
                if layer == 0:
                    v.wait_ge(far_in, 16 * FAR_LOADS)
                    v.scalar_tensor_tensor(g0, far["keys_t"], 2.0, far["rw_t"], ALU.mult, ALU.add)
                    v.scalar_tensor_tensor(key2, far["keys_t"], -1.0, far["keys_t"], ALU.mult, ALU.mult)\
                     .then_inc(g_const, 1)
                    v.wait_ge(g_psum, base["psum"] + 1)
                    c.step(v.tensor_tensor(g0b, bank[3][:, 0:E], far["rb"], ALU.add)).settle()
                    c.step(v.tensor_tensor(wsum, mv[:, :, 1], rstd, ALU.mult)).settle()
                    c.step(v.tensor_tensor(wsum, wsum, rstd, ALU.mult)).settle()
                L = logits[:, :, 0:E]
                got = bank[2][:, 0:TILES * E].rearrange("p (t e) -> p t e", e=E)
                v.wait_ge(g_psum, base["psum"] + (1 if layer else 2))
                if layer == 0:
                    c.step(v.tensor_tensor(L, got, g0b.unsqueeze(1).to_broadcast([P, TILES, E]), ALU.add)).settle()
                    c.step(v.scalar_tensor_tensor(L, wide(wsum), -float(D), L, ALU.mult, ALU.add)).settle()
                elif layer == 1:
                    c.step(v.tensor_tensor(L, got, far["lb1"].unsqueeze(1).to_broadcast([P, TILES, E]), ALU.add))
                    c.settle()
                    v.tensor_scalar(hit[:, :, 0:E], L, -1.0, None, ALU.mult).then_inc(g_val, 1)
                    v.wait_ge(g_exp, base["exp"] + 1)
                    c.step(v.tensor_scalar(hitw[:, :, 0:E], hitw[:, :, 0:E], 1.0, None, ALU.add)).settle()
                    c.step(v.reciprocal(L, hitw[:, :, 0:E])).settle()
                else:
                    c.step(v.tensor_copy(L, got)).settle()
                for t in range(TILES):
                    last = v.max(top8[:, t, :], logits[:, t, 0:E])
                c.step(last).settle()
                for t in range(TILES):
                    last = v.max_index(index[:, t, :], top8[:, t, :], logits[:, t, 0:E])
                c.step(last).settle()
                c.step(v.tensor_copy(indexf, index)).settle()
                w = wk[:, :, 0:K]
                if layer == 1:
                    c.step(v.tensor_tensor(wsum, top8[:, :, 0], top8[:, :, 1], ALU.add)).settle()
                    c.step(v.tensor_scalar(wsum, wsum, 1e-8, None, ALU.add)).settle()
                    source = top8
                else:
                    v.tensor_tensor(w, top8[:, :, 0:K], top8[:, :, 0:1].to_broadcast([P, TILES, K]), ALU.subtract)\
                     .then_inc(g_val, 1)
                    v.wait_ge(g_exp, base["exp"] + 1)
                    c.step(v.tensor_reduce(wsum, w, AX.X, ALU.add)).settle()
                    source = wk
                c.step(v.reciprocal(wrec, wsum)).settle()
                c.step(v.tensor_tensor(w, source[:, :, 0:K], wrec.unsqueeze(2).to_broadcast([P, TILES, K]), ALU.mult))
                c.settle()
                G, C, Hh, Hw = gates[:, :, 0:E], chosen[:, :, 0:E], hit[:, :, 0:E], hitw[:, :, 0:E]
                slots = far["at"][:, 0:E].unsqueeze(1).to_broadcast([P, TILES, E])
                for k in range(K):
                    first = k == 0
                    Ht = C if first and layer == 1 else Hh
                    c.step(v.tensor_tensor(Ht, slots, wide(indexf[:, :, k]), ALU.is_equal)).settle()
                    c.step(v.tensor_tensor(G if first else Hw, Ht, wide(wk[:, :, k]), ALU.mult)).settle()
                    if not first:
                        c.step(v.tensor_tensor(G, G, Hw, ALU.add)).settle()
                        if layer == 1:
                            c.step(v.tensor_tensor(C, C, Hh, ALU.add)).settle()
                if layer == 1:
                    v.tensor_reduce(sums[:, 0:E], G.rearrange("p t e -> p e t"), AX.X, ALU.add)
                    v.tensor_reduce(sums[:, E:2 * E], C.rearrange("p t e -> p e t"), AX.X, ALU.add).then_inc(g_ready, 2)
                    v.wait_ge(g_psum, base["psum"] + 2)
                    c.step(v.tensor_scalar(wmean[0:E, 0:1], bank[3][0:E, 1:2], 1.0, None, ALU.max)).settle()
                    c.step(v.reciprocal(wmean[0:E, 1:2], wmean[0:E, 0:1])).settle()
                    c.step(v.tensor_tensor(wmean[0:E, 2:3], bank[3][0:E, 0:1], wmean[0:E, 1:2], ALU.mult)).settle()
                    v.tensor_scalar(expert1[0:E], far["expert"][0:E, 0:E // 2, :], wmean[0:E, 2:3], None, ALU.mult)\
                     .then_inc(g_const, 1)
                else:
                    c.settle()
                    c.step(v.tensor_copy(hit[:, :, 0:E], G)).settle()
                    v.tensor_copy(wsum, wsum).then_inc(g_ready, 1)
                if layer == 0:
                    for k in range(CHUNKS):
                        v.wait_ge(g_psum, base["psum"] + 3 + k)
                        xs = x[:, CT * k:CT * k + CT, :]
                        v.tensor_tensor(xs, xs, bank[k][:, :].rearrange("p (t d) -> p t d", d=D), ALU.add)\
                         .then_inc(x_done, 1)

            def scalar(act):
                act.wait_ge(g_val, base["val"] + 1)
                if layer == 1:
                    act.activation(hitw[:, :, 0:E], hit[:, :, 0:E], ACT.Exp).then_inc(g_exp, 1)
                else:
                    act.activation(wk[:, :, 0:K], wk[:, :, 0:K], ACT.Exp).then_inc(g_exp, 1)
                for k in range(CHUNKS):
                    act.wait_ge(g_turned, base["turned"] + k + 1)
                    act.activation(gates_t[0:E, k * CHUNK:(k + 1) * CHUNK], bank[4 + k][0:E, :], ACT.Copy)\
                       .then_inc(g_t, 1)

            def tensor(pe):
                if layer == 0:
                    pe.wait_ge(g_const, base["const"] + 1)
                    pe.matmul(bank[3][:, 0:E], ones, key2, start=True, stop=True).then_inc(g_psum, 1)
                else:
                    pe.wait_ge(far_in, 16 * FAR_LOADS)
                for t in range(TILES):
                    if t % CT == 0:
                        pe.wait_ge(nrm_xt, at_t - CHUNKS + t // CT + 1)
                    last = pe.matmul(bank[2][:, t * E:(t + 1) * E], xn_t[:, t * P:(t + 1) * P], weights[:, 0:E],
                                     start=True, stop=True)
                last.then_inc(g_psum, 1)
                pe.wait_ge(g_ready, base["ready"] + (2 if layer == 1 else 1))
                if layer == 1:
                    pe.matmul(bank[3][0:E, 0:1], sums[:, 0:E], ones[:, 0:1], start=True, stop=True)
                    pe.matmul(bank[3][0:E, 1:2], sums[:, E:2 * E], ones[:, 0:1], start=True, stop=True)\
                      .then_inc(g_psum, 1)
                source = chosen if layer == 1 else gates
                for k in range(CHUNKS):
                    for j in range(CT):
                        last = pe.transpose(bank[4 + k][0:E, j * P:(j + 1) * P], source[:, CT * k + j, 0:E], eye)
                    last.then_inc(g_turned, 1)
                if layer == 0:
                    for k in range(CHUNKS):
                        pe.wait_ge(g_t, base["turned"] + k + 1)
                        for j in range(CT):
                            t = CT * k + j
                            last = pe.matmul(bank[k][:, j * P:(j + 1) * P], gates_t[0:E, t * P:(t + 1) * P],
                                             far["b2"][0:E, :], start=True, stop=True)
                        last.then_inc(g_psum, 1)

            programs["vector"].append(vector)
            programs["scalar"].append(scalar)
            programs["tensor"].append(tensor)
            return base["turned"] + CHUNKS

        SCORES_AHEAD = 7
        MIX_BEHIND = 3
        PROJECT_AT = {12: list(range(12)), 5: [1, 3, 5, 7, 11]}
        OUT_AT = {12: [3, 4, 6, 7, 8], 5: [3, 4]}

        MASKS_AT = [1, 13]

        def plan(first, last, jobs):
            project_at, out_at = PROJECT_AT[jobs], OUT_AT[jobs]
            for n in range(H):
                g, j = divmod(n, HG)
                ahead = divmod(n + SCORES_AHEAD, H)
                cut = ((g + 1) // GROUPS, (g + 1) % GROUPS, 0)
                if not (last and ahead[0]):
                    yield "scores", ahead[0], *divmod(ahead[1], HG)
                if j == 0 and not (last and cut[0]):
                    yield "cut", *cut
                if not last:
                    if n in project_at:
                        yield "project", 1, project_at.index(n), 0
                    if n - 1 in project_at:
                        yield "split", 1, project_at.index(n - 1), 0
                    if n in MASKS_AT:
                        yield "masks", 1, MASKS_AT.index(n), 0
                yield "weigh", 0, g, j
                if n >= MIX_BEHIND:
                    yield "mix", 0, *divmod(n - MIX_BEHIND, HG)
                elif not first:
                    yield "mix", -1, *divmod(H + n - MIX_BEHIND, HG)
                if n == MIX_BEHIND - 1 and not first:
                    yield "gather", -1, 0, 0
                if not first and n in out_at:
                    k = out_at.index(n)
                    yield ("turn_out", -1, k, 0) if k < len(out_at) - 1 else ("out", -1, 0, 0)
                if j == 1 and not (last and cut[0]):
                    yield "maxima", *cut

        def opening(jobs):
            yield "masks", 0, 0, 0
            yield "masks", 0, 1, 0
            for k in range(jobs + 1):
                if k < jobs:
                    yield "project", 0, k, 0
                if k >= 1:
                    yield "split", 0, k - 1, 0
            for n in range(SCORES_AHEAD):
                yield "scores", 0, *divmod(n, HG)
                if n == HG - 1:
                    yield "cut", 0, 0, 0
            yield "maxima", 0, 0, 0

        def close(jobs):
            for n in range(H - MIX_BEHIND, H):
                yield "mix", 0, *divmod(n, HG)
            yield "gather", 0, 0, 0
            for k in range(len(OUT_AT[jobs]) - 1):
                yield "turn_out", 0, k, 0
            yield "out", 0, 0, 0

        def walk(eng, steps, jobs, chain=None):
            def take_steps(order, at):
                for name, ahead, g, j in order:
                    if name in steps:
                        steps[name](eng, at.move(ahead), g, j)
            take_steps(opening(jobs), Seq(0, 0))
            take_steps(plan(True, False, jobs), Seq(0, 0))
            with eng.Fori(0, B // 2 - 1) as i:
                if chain:
                    chain.turn(i, steps["chained"])
                take_steps(plan(False, False, jobs), Seq(i, 1))
                take_steps(plan(False, False, jobs), Seq(i + 1, 0))
                if chain:
                    chain.turned(B // 2 - 1)
            take_steps(plan(False, True, jobs), Seq(B // 2 - 1, 1))
            take_steps(close(jobs), Seq(B // 2 - 1, 1))

        def attention(layer, need_t):
            wide = layer == 0
            masked = layer < 3
            L = f"a{layer}_"
            s = {k: sem(L + k) for k in (
                "projected",
                "evacuated",
                "halved",
                "scored",
                "maxed",
                "cut",
                "turned",
                "freed",
                "shifts",
                "weighed",
                "biased",
                "exps",
                "probs",
                "mixed",
                "gathered",
                "masks",
                "att_t",
                "vready",
            )}
            ctx_in = [sem(L + f"ctx_in{p}") for p in range(2)]
            mask_in = [sem(L + f"mask_in{p}") for p in range(2)]
            x0 = x_steps[0]
            x_steps[0] += B
            pads = 2

            top[0] = phases if wide else body
            if wide:
                qh, ql, kh, kl = ([take([PAIRS, S], F16) for _ in range(2)] for _ in range(4))
            ctx_t = [take([S]) for _ in range(2)]
            x32 = take([2, 2 * S])
            exps = take([HG, 2 * S])
            p_high = take([HG, 2 * S], F16)
            p_low = take([HG, 2 * S], F16)
            biased = take([2, 2 * S]) if masked else None
            row_max = take([2, SB, HG])
            parts = take([SB, P], BF16)
            part_of = parts.rearrange("p m (j r) -> p m j r", r=P // HG)
            shift = take([2, S], BF16)
            if wide:
                wq, wk0, wv, wo = take([1024]), take([1024]), take([1024]), take([PAIRS, D])
                bias_t = take([H, 2 * S])
                bias_q = take([H, 2 * S], BF16)
                rden = take([2, 2, SB])
                att = [take([SB, H * DH0]) for _ in range(2)]
                att_t = take([PAIRS, S])
                raw = [take([2, 2 * S], U8) for _ in range(2)]
                add_t = [take([2 * S], BF16) for _ in range(2)]
                add_q = [take([2 * S], BF16) for _ in range(2)]
            else:
                wq, wk0, wv, wo = (far[f"w{c}{layer}"] for c in "qkvo")
                bq, bk, bv, bo = (far[f"b{c}{layer}"] for c in "qkvo")
                high = take([2, 2 * S], F16)
                spread = take([2, S], F16)
                qs = [take([GROUPS * HG, S], F16).rearrange("p (g j) s -> p g j s", j=HG) for _ in range(2)]
                ks = [take([GROUPS, S], F16) for _ in range(2)]
                rden = take([SB, H])
                att = [take([SB, D]) for _ in range(2)]
                att_t = take([1, S])
                bqs = take([HG])
                if layer == 1:
                    raw_m = take([2, 2 * S], I32)
                    raw_b = take([2, 2 * S])
                    low = take([2 * S])
                    add_t = [take([2 * S]) for _ in range(2)]
                    add_q = [take([2 * S], BF16) for _ in range(2)]
            if not wide:
                assert top[0] <= 36800
            hd = DH0 if wide else DH
            VS = hd + 2
            val = [take([SB, 2, H * VS], F16) for _ in range(2)]
            OT = PAIRS // 2 if wide else 1
            S_BANK, W_BANK, O_BANK, PR, TR = (0, 1), (2, 3), (4, 5), 6, 7
            JOBS = 12 if wide else 5
            QK_JOBS = 8 if wide else 4
            AHEAD = 0 if wide else 1

            def head(q, g, j):
                return q.b * H + HG * g + j

            def group(q, g):
                return q.b * GROUPS + g

            def tr_places(order):
                return {(name, g): k for k, (name, _, g, _) in
                        enumerate(t for t in order if t[0] in ("maxima", "turn_out", "out"))}

            TR_FIRST, TR_TURN, TR_LAST = (tr_places(plan(f, l, JOBS)) for f, l in ((1, 0), (0, 0), (0, 1)))
            TR_CLOSE = tr_places(close(JOBS))

            def tr_job(name, q, g=0):
                r = q.b - (0 if g else 1) if name == "maxima" else q.b + 1
                if not isinstance(r, int):
                    return (r - 1) * len(TR_TURN) + (1 + len(TR_FIRST) + TR_TURN[name, g])
                if r < 0:
                    return 0
                if r == 0:
                    return 1 + TR_FIRST[name, g]
                before = 1 + len(TR_FIRST) + (min(r, B - 1) - 1) * len(TR_TURN)
                if r < B:
                    return before + (TR_LAST if r == B - 1 else TR_TURN)[name, g]
                return before + len(TR_LAST) + TR_CLOSE[name, g]

            def both_banks(q):
                return isinstance(q.b, int) and q.b == 0

            def project_bank(q, k):
                return bank[O_BANK[0] if both_banks(q) and k % 2 else PR]

            def part_tiles(q, k):
                if wide and k < QK_JOBS:
                    kind, pair = divmod(k, 4)
                    return ([w[q.p][:, 2 * pair:2 * pair + 2, :] for w in ((qh, ql), (kh, kl))[kind]],
                            project_bank(q, k)[:, :].rearrange("p (c s) -> p c s", s=S))
                if wide:
                    t, hf = divmod(k - QK_JOBS, 2)
                    n = H // 2
                    return ([val[q.p][:, t, c, hf * n * VS:(hf + 1) * n * VS].rearrange("p (h c) -> p h c", c=VS)[:, :, 0:hd]
                             for c in range(2)], project_bank(q, k)[:, :].rearrange("p (h d) -> p h d", d=hd))
                return ([val[q.p][:, :, c, :].rearrange("p t (h c) -> p t h c", c=VS)[:, :, :, 0:hd] for c in range(2)],
                        project_bank(q, k)[:, 0:SB * D].rearrange("p (t h d) -> p t h d", h=H, d=hd))

            def like(flat, tile):
                n = int(np.prod(tile.shape[1:]))
                if len(tile.shape) == 3:
                    return flat[:, 0:n].rearrange("p (a b) -> p a b", b=tile.shape[2])
                return flat[:, 0:n].rearrange("p (a b c) -> p a b c", b=tile.shape[2], c=tile.shape[3])

            def sync(sp):
                if wide:
                    sp.dma_start(ctx_t[0], io["ctx_t"][:, 0:S]).then_inc(ctx_in[0], 16)
                    for tile, name in ((wq, "wq0"), (wk0, "wk0"), (wv, "wv0"), (wo, "wo0")):
                        sp.dma_start(tile, io[name]).then_inc(w0_in, 16)
                else:
                    wait(sp, x_done, x0)

                def masks(i, p):
                    if wide:
                        for k, name in enumerate(("mask0_t", "mask0_q")):
                            sp.dma_start(raw[p][:, k, :], io[name][bass.ds(i * 2 + p, 1)].rearrange("b p c -> p (b c)"))\
                              .then_inc(mask_in[p], 16)
                    elif layer == 1:
                        if not isinstance(i, int):
                            wait_alone(sp, s["masks"], (i * 2 + p) * 2, sp_step)
                        elif p:
                            sp.wait_ge(s["masks"], p * 2)
                        for k, name in enumerate(("t", "q")):
                            for tile, kind in ((raw_m, "mask1_"), (raw_b, "bias1_")):
                                sp.dma_start(tile[:, k, :], io[kind + name][bass.ds(i * 2 + p, 1)].rearrange("b p c -> p (b c)"))\
                                  .then_inc(mask_in[p], 16)

                def contexts(i, p):
                    sp.dma_start(ctx_t[p], io["ctx_t"][:, bass.ds((i * 2 + p) * S, S)]).then_inc(ctx_in[p], 16)

                if not wide:
                    contexts(0, 0)
                masks(0, 0)
                contexts(0, 1)
                if wide:
                    for g in range(GROUPS):
                        sp.dma_start(bias_t[:, HG * g:HG * g + HG, :], io["bias0_t"][:, HG * g:HG * g + HG, :])\
                          .then_inc(biast_in[g], 16)
                masks(0, 1)
                with sp.Fori(1, B // 2) as i:
                    for p in range(2):
                        wait_alone(sp, s["projected"], (i * 2 + p - 1) * JOBS, sp_step)
                        contexts(i, p)
                        if wide:
                            wait_alone(sp, s["masks"], (i * 2 + p - 1) * 2, sp_step)
                        masks(i, p)

            def pool(g):
                if wide:
                    for k in range(GROUPS):
                        g.dma_start(bias_q[:, HG * k:HG * k + HG, :], io["bias0_q"][:, HG * k:HG * k + HG, :])\
                         .then_inc(biasq_in[k], 16)
                else:
                    g.wait_ge(x_done, x0)
                for p in range(2):
                    if not wide:
                        g.memset(qs[p], 0.0)
                    g.memset(val[p], 0.0).then_inc(s["vready"], 1)
                g.wait_ge(s["vready"], 2)
                for p in range(2):
                    g.memset(val[p][:, :, 0, :].rearrange("p t (h c) -> p t h c", c=VS)[:, :, :, hd:hd + 1], 1.0)\
                     .then_inc(s["vready"], 1)

                def split_(g_, q, k, _):
                    g_.wait_ge(s["evacuated"], q.b * JOBS + k + 1)
                    to, _ = part_tiles(q, k)
                    g_.tensor_tensor(to[1], like(x32[:, k % 2, :], to[1]), to[0], ALU.subtract).then_inc(s["halved"], 1)

                def weigh(g_, q, g, j):
                    g_.wait_ge(s["exps"], head(q, g, j) * 2 + 2)
                    g_.tensor_tensor(p_low[:, j, :], exps[:, j, :], p_high[:, j, :], ALU.subtract)\
                      .then_inc(s["probs"], 1)

                steps = {"weigh": weigh}
                if wide:
                    steps["split"] = split_
                walk(g, steps, JOBS)

            def tensor(pe):
                if wide:
                    pe.wait_ge(eyes_ready, 3)
                    pe.wait_ge(w0_in, 64)
                    pe.wait_ge(nrm_xt, CHUNKS * need_t)
                else:
                    pe.wait_ge(far_in, 16 * FAR_LOADS)
                    pe.wait_ge(nrm_xt, CHUNKS * need_t)

                def project(pe, q, k, _):
                    wait(pe, s["evacuated"], q.b * JOBS + k - both_banks(q))
                    if k == 0:
                        pe.wait_ge(ctx_in[q.p], q.i * 16 + 16)
                    bk_ = project_bank(q, k)
                    xt = xn_t[:, bass.ds(q.b * S, S)]
                    ct = ctx_t[q.p]
                    if k < (8 if wide else 4):
                        kind, pair = divmod(k, 4 if wide else 2)
                        w = (wq, wk0)[kind]
                        for c in range(2):
                            m = 2 * pair + c
                            lhs = w[:, m * P:(m + 1) * P] if wide else w[:, m, :]
                            last = pe.matmul(bk_[:, c * S:(c + 1) * S], lhs, ct if kind else xt, start=True, stop=True)
                    elif wide:
                        t, hf = divmod(k - 8, 2)
                        last = pe.matmul(bk_[:, :], ct[:, t * P:(t + 1) * P], wv[:, hf * 512:(hf + 1) * 512],
                                         start=True, stop=True)
                    else:
                        for t in range(SB):
                            o = bk_[:, t * P:(t + 1) * P]
                            pe.matmul(o, ct[:, t * P:(t + 1) * P], wv, start=True, stop=False)
                            last = pe.matmul(o, ones[0:1, :], bv[0:1, :], start=False, stop=True)
                    last.then_inc(s["projected"], 1)

                def scores(pe, q, g, j):
                    n = head(q, g, j)
                    wait(pe, s["maxed"], n - 1)
                    if g == 0 and j == 0:
                        if wide:
                            pe.wait_ge(s["evacuated"], q.b * JOBS + QK_JOBS)
                        else:
                            pe.wait_ge(s["halved"], q.b * JOBS + QK_JOBS + AHEAD)
                        if masked:
                            pe.wait_ge(s["masks"], q.b * 2 + 1)
                    sc = bank[S_BANK[j % 2]]
                    if wide:
                        if isinstance(q.b, int) and q.b == 0 and j == 0:
                            pe.wait_ge(biasq_in[g], 16)
                        r, t = 64 * (j % 2), 2 * g + j // 2
                        pe.matmul(sc[:, :], eye16, bias_q[:, HG * g + j, :], start=True, stop=False, skip_group_check=True)
                        pe.matmul(sc[:, :], eye16, add_q[q.p], start=False, stop=False, skip_group_check=True)
                        for m in range(SB):
                            last = pe.matmul(sc[:, m * S:(m + 1) * S], qh[q.p][r:r + DH0, t, m * P:(m + 1) * P],
                                             kh[q.p][r:r + DH0, t, :], start=False, stop=m == 1, skip_group_check=True)
                    else:
                        if masked:
                            pe.matmul(sc[:, :], eye16, add_q[q.p], start=True, stop=False, skip_group_check=True)
                        for m in range(SB):
                            last = pe.matmul(sc[:, m * S:(m + 1) * S], qs[q.p][:, g, j, m * P:(m + 1) * P],
                                             ks[q.p][:, g, :], start=not masked, stop=True,
                                             skip_group_check=masked)
                    last.then_inc(s["scored"], 1)

                def maxima(pe, q, g, _):
                    pe.wait_ge(s["cut"], group(q, g) * 2 + 2)
                    job = tr_job("maxima", q, g)
                    wait(pe, s["freed"], job)
                    to = bank[TR][:, 0:S // 2].bitcast(BF16)
                    for m in range(SB):
                        last = pe.transpose(to[:, m * P:(m + 1) * P], parts[:, m, :], eye16)
                    last.then_inc(s["turned"], 1)

                def weigh(pe, q, g, j):
                    n = head(q, g, j)
                    if masked:
                        wait(pe, s["biased"], n - 1)
                    else:
                        wait(pe, s["exps"], n * 2 - 2)
                    if j == 0:
                        pe.wait_ge(s["shifts"], group(q, g) + 1)
                    if wide and g == 0 and j == 0:
                        pe.wait_ge(s["halved"], q.b * JOBS + QK_JOBS)
                        pe.wait_ge(s["masks"], q.b * 2 + 2)
                    o = bank[W_BANK[j % 2]]
                    sh = shift[:, g % 2, :].unsqueeze(1).to_broadcast([P, SB, S])
                    if wide:
                        r, t = 64 * (j % 2), 2 * g + j // 2
                        pe.matmul(o[:, :], eye16, add_t[q.p], start=True, stop=False, skip_group_check=True)
                        pe.matmul(o[:, :], drop[:, j, :], sh, start=False, stop=False, skip_group_check=True)
                        for m in range(SB):
                            c = o[:, m * S:(m + 1) * S]
                            for a, b_ in ((kh, qh), (kl, qh), (kh, ql)):
                                last = pe.matmul(c, a[q.p][r:r + DH0, t, m * P:(m + 1) * P], b_[q.p][r:r + DH0, t, :],
                                                 start=False, stop=m == 1 and b_ is ql, skip_group_check=True)
                    else:
                        pe.matmul(o[:, :], drop[:, j, :], sh, start=True, stop=False, skip_group_check=True)
                        for m in range(SB):
                            last = pe.matmul(o[:, m * S:(m + 1) * S], ks[q.p][:, g, m * P:(m + 1) * P],
                                             qs[q.p][:, g, j, :], start=False, stop=m == 1, skip_group_check=True)
                    last.then_inc(s["weighed"], 1)

                def mix(pe, q, g, j):
                    n = head(q, g, j)
                    pe.wait_ge(s["probs"], n + 1)
                    h = HG * g + j
                    if h == 0:
                        pe.wait_ge(s["halved"], q.b * JOBS + JOBS + AHEAD)
                    if wide:
                        if j % 2 == 0:
                            wait(pe, s["gathered"], q.b * PAIRS + h // 2 - 1)
                        o, first, base = bank[O_BANK[(h // 2) % 2]], j % 2 == 0, (j % 2) * SB
                    else:
                        if h == 0:
                            wait(pe, s["gathered"], q.b)
                        o, first, base = bank[O_BANK[q.p]], h == 0, 0
                    vh, vl = (val[q.p][:, :, k, h * VS:(h + 1) * VS] for k in range(2))
                    for m in range(SB):
                        at = (base + m) * VS if wide else (m * H + h) * VS
                        for t in range(SB):
                            keys = slice(t * S + m * P, t * S + (m + 1) * P)
                            for k, (a, b_) in enumerate(((p_high, vh), (p_high, vl), (p_low, vh))):
                                last = pe.matmul(o[:, at:at + VS], a[:, j, keys], b_[:, t, :],
                                                 start=first and m == 0 and t == 0 and k == 0, stop=t == 1 and k == 2,
                                                 skip_group_check=True)
                    last.then_inc(s["mixed"], 1)

                def turn_out(pe, q, k, _):
                    wait(pe, s["freed"], tr_job("turn_out", q, k))
                    if k == 0:
                        pe.wait_ge(s["gathered"], q.b * PAIRS + PAIRS if wide else q.b + 2)
                    for c in range(2 if wide else 1):
                        n = 2 * k + c
                        for m in range(SB):
                            last = pe.transpose(bank[TR][:, (c * SB + m) * P:(c * SB + m + 1) * P],
                                                att[q.p][:, m, n * P:(n + 1) * P], eye)
                    last.then_inc(s["turned"], 1)

                def out(pe, q, _, __):
                    pe.wait_ge(s["att_t"], q.b * OT + OT)
                    wait(pe, s["freed"], tr_job("out", q))
                    for m in range(SB):
                        o = bank[TR][:, m * P:(m + 1) * P]
                        if wide:
                            for t in range(PAIRS):
                                last = pe.matmul(o, att_t[:, t, m * P:(m + 1) * P], wo[:, t, :],
                                                 start=t == 0, stop=t == PAIRS - 1)
                        else:
                            pe.matmul(o, att_t[:, 0, m * P:(m + 1) * P], wo, start=True, stop=False)
                            last = pe.matmul(o, ones[0:1, :], bo[0:1, :], start=False, stop=True)
                    last.then_inc(s["turned"], 1)

                walk(pe, {"project": project, "scores": scores, "maxima": maxima, "weigh": weigh, "mix": mix, "turn_out": turn_out,
                          "out": out}, JOBS)

            def scalar(act):
                if not wide:
                    act.wait_ge(far_in, 16 * FAR_LOADS)
                    act.wait_ge(s["halved"], 1)

                def project(act, q, k, _):
                    act.wait_ge(s["projected"], q.b * JOBS + k + 1)
                    wait(act, s["halved"], q.b * JOBS + k - 1 + AHEAD)
                    copy = x32[:, (q.p * JOBS + k) % 2, :]
                    b_ = project_bank(q, k)
                    if wide or k >= QK_JOBS:
                        if k == 0:
                            wait(act, s["weighed"], q.b * H - H)
                        if k == QK_JOBS:
                            act.wait_ge(s["vready"], 4)
                            wait(act, s["mixed"], q.b * H - H)
                        scale = DH0 ** -0.5 if wide and k < QK_JOBS // 2 else 1.0
                        to, src = part_tiles(q, k)
                        act.activation(like(copy, to[0]), src, ACT.Copy, scale=scale)
                        last = act.activation(to[0], src, ACT.Copy, scale=scale)
                    else:
                        kind, pair = divmod(k, 2)
                        for c in range(2):
                            m = 2 * pair + c
                            bias = (bqs if kind == 0 else bk)[:, m:m + 1]
                            last = act.activation(copy[:, c * S:(c + 1) * S], b_[:, c * S:(c + 1) * S], ACT.Identity,
                                                  bias=bias, scale=DH ** -0.5 if kind == 0 else 1.0)
                    last.then_inc(s["evacuated"], 1)

                def maxima(act, q, g, _):
                    act.wait_ge(s["turned"], tr_job("maxima", q, g) + 1)
                    wait(act, s["weighed"], group(q, g) * HG - HG)
                    act.activation(shift[:, g % 2, :], bank[TR][:, 0:S // 2].bitcast(BF16), ACT.Copy)\
                       .then_inc(s["shifts"], 1)
                    act.wait_ge(s["shifts"], group(q, g) + 1)
                    act.sem_inc(s["freed"], 1)

                def weigh(act, q, g, j):
                    n = head(q, g, j)
                    act.wait_ge(s["biased" if masked else "weighed"], n + 1)
                    wait(act, s["mixed"], n - 3)
                    src = biased[:, j % 2, :] if masked else bank[W_BANK[j % 2]][:, :]
                    act.activation(exps[:, j, :], src, ACT.Exp).then_inc(s["exps"], 1)
                    act.activation(p_high[:, j, :], src, ACT.Exp).then_inc(s["exps"], 1)

                def turn_out(act, q, k, _):
                    act.wait_ge(s["turned"], tr_job("turn_out", q, k) + 1)
                    n = 2 if wide else 1
                    act.activation(att_t[:, n * k:n * k + n, :], bank[TR][:, 0:n * S].rearrange("p (n c) -> p n c", c=S),
                                   ACT.Copy).then_inc(s["att_t"], 1)
                    act.wait_ge(s["att_t"], q.b * OT + k + 1)
                    act.sem_inc(s["freed"], 1)

                walk(act, {"project": project, "maxima": maxima, "weigh": weigh, "turn_out": turn_out}, JOBS)

            def vector(v):
                c = dve(v)
                if wide:
                    v.wait_ge(w0_in, 64)
                    c.step(v.memset(parts, 0.0)).settle()
                else:
                    v.wait_ge(far_in, 16 * FAR_LOADS)
                    c.step(v.memset(parts, 0.0)).settle()
                    v.tensor_scalar(bqs, bq, DH ** -0.5, None, ALU.mult).then_inc(s["halved"], 1)
                    v.sem_inc(s["gathered"], 1)

                def masks(v, q, k, _):
                    if not masked:
                        return
                    to = (add_q, add_t)[k][q.p]
                    if wide:
                        v.wait_ge(mask_in[q.p], q.i * 32 + 32)
                        if k == 1:
                            wait(v, s["weighed"], q.b * H - H)
                        last = v.tensor_scalar(to, raw[q.p][:, 1 - k, :], 0.0, -BIG, ALU.is_equal, ALU.mult)
                    else:
                        v.wait_ge(mask_in[q.p], q.i * 64 + 64)
                        wait(v, s["masks"], q.b * 2 + k)
                        if k == 0:
                            wait(v, s["scored"], q.b * H - H)
                        c.step(v.tensor_scalar(low, raw_m[:, 1 - k, :], 0.0, -BIG, ALU.is_equal, ALU.mult)).settle()
                        last = v.tensor_tensor(to, low, raw_b[:, 1 - k, :], ALU.add)
                    last.then_inc(s["masks"], 1)

                def split_(v, q, k, _):
                    v.wait_ge(s["evacuated"], q.b * JOBS + k + 1)
                    n = (q.p * JOBS + k) % 2
                    if k == QK_JOBS:
                        to, _ = part_tiles(q, k)
                        v.tensor_tensor(to[1], like(x32[:, n, :], to[1]), to[0], ALU.subtract).then_inc(s["halved"], 1)
                        return
                    if k == 0:
                        wait(v, s["vready"], 2)
                    kind, pair = divmod(k, 2)
                    c.step(v.tensor_copy(high[:, n, :], x32[:, n, :])).settle()
                    if k == 0:
                        wait(v, s["weighed"], q.b * H - H)
                    to = (spread, ks[q.p][:, 2 * pair:2 * pair + 2, :])[kind]
                    last = v.scalar_tensor_tensor(to, high[:, n, :].rearrange("p (a b) -> p a b", b=S), split[:, kind:kind + 1],
                                                  x32[:, n, :].rearrange("p (a b) -> p a b", b=S), ALU.mult, ALU.add)
                    if kind == 0:
                        c.step(last).settle()
                        for j in range(HG):
                            rows = slice(j * P // HG, (j + 1) * P // HG)
                            last = v.tensor_copy(qs[q.p][rows, 2 * pair:2 * pair + 2, j, :], spread[rows])
                    last.then_inc(s["halved"], 1)

                def scores(v, q, g, j):
                    v.wait_ge(s["scored"], head(q, g, j) + 1)
                    v.tensor_reduce(row_max[:, g % 2, :, j], bank[S_BANK[j % 2]][:, :].rearrange("p (m c) -> p m c", c=S),
                                    AX.X, ALU.max).then_inc(s["maxed"], 1)

                def cut(v, q, g, _):
                    v.wait_ge(s["maxed"], group(q, g) * HG + HG)
                    if not (isinstance(q.b, int) and q.b == g == 0):
                        v.wait_ge(s["turned"], 1 + (tr_job("maxima", q, g - 1) if g else tr_job("maxima", q.move(-1), GROUPS - 1)))
                    rm = row_max[:, g % 2, :, :]
                    c.step(v.tensor_scalar(rm, rm, FLOOR, LIFT, ALU.max, ALU.subtract)).settle()
                    v.tensor_copy(part_of[:, :, :, 0], rm).then_inc(s["cut"], 1)
                    v.wait_ge(s["cut"], group(q, g) * 2 + 1)
                    v.tensor_tensor(part_of[:, :, :, 1], rm, part_of[:, :, :, 0], ALU.subtract).then_inc(s["cut"], 1)

                def weigh(v, q, g, j):
                    if not masked:
                        return
                    n = head(q, g, j)
                    v.wait_ge(s["weighed"], n + 1)
                    wait(v, s["exps"], n * 2 - 2)
                    if not wide and g == 0 and j == 0:
                        v.wait_ge(s["masks"], q.b * 2 + 2)
                    if wide:
                        if isinstance(q.b, int) and q.b == 0 and j == 0:
                            v.wait_ge(biast_in[g], 16)
                        add = bias_t[:, HG * g + j, :]
                    else:
                        add = add_t[q.p]
                    v.tensor_tensor(biased[:, j % 2, :], bank[W_BANK[j % 2]][:, :], add, ALU.add).then_inc(s["biased"], 1)

                def mix(v, q, g, j):
                    if not wide or j % 2 == 0:
                        return
                    pair = 2 * g + j // 2
                    v.wait_ge(s["mixed"], head(q, g, j) + 1)
                    o = bank[O_BANK[pair % 2]]
                    o = o[:, 0:2 * SB * VS].rearrange("p (j m c) -> p j m c", j=2, c=VS)
                    rd = rden[:, pair % 2]
                    wait(v, s["gathered"], q.b * PAIRS + pair - 1)
                    c.step(v.tensor_scalar(rd, o[:, :, :, hd], 1 / BIG, None, ALU.max)).settle()
                    c.step(v.reciprocal(rd, rd)).settle()
                    to = att[q.p].rearrange("p m (h d) -> p h m d", d=hd)[:, 2 * pair:2 * pair + 2]
                    v.tensor_tensor(to, o[:, :, :, 0:hd], rd.unsqueeze(3).to_broadcast([P, 2, SB, hd]), ALU.mult)\
                     .then_inc(s["gathered"], 1)

                def gather(v, q, _, __):
                    if wide:
                        return
                    v.wait_ge(s["mixed"], q.b * H + H)
                    o = bank[O_BANK[q.p]][:, 0:SB * H * VS].rearrange("p (m h c) -> p m h c", h=H, c=VS)
                    c.step(v.reciprocal(rden, o[:, :, :, hd])).settle()
                    v.tensor_tensor(att[q.p].rearrange("p m (h d) -> p m h d", d=hd), o[:, :, :, 0:hd],
                                    rden.unsqueeze(3).to_broadcast([P, SB, H, hd]), ALU.mult).then_inc(s["gathered"], 1)

                def out(v, q, _, __):
                    v.wait_ge(s["turned"], tr_job("out", q) + 1)
                    xs = x[:, bass.ds(q.b * SB, SB), :]
                    v.tensor_tensor(xs, bank[TR][:, 0:S].rearrange("p (t d) -> p t d", d=D), xs, ALU.add)\
                     .then_inc(x_done, 1)
                    v.wait_ge(x_done, q.b + 1 + x0)
                    v.sem_inc(s["freed"], 1)

                steps = {"masks": masks, "scores": scores, "cut": cut, "weigh": weigh,
                         "mix": mix, "gather": gather, "out": out,
                         "chained": 2 * (GROUPS + (2 * PAIRS if wide else 7 + (2 if layer == 1 else 0)))}
                if not wide:
                    steps["split"] = split_
                walk(v, steps, JOBS, c)

            programs["sync"].append(sync)
            programs["gpsimd"].append(pool)
            programs["tensor"].append(tensor)
            programs["scalar"].append(scalar)
            programs["vector"].append(vector)

        def experts0(gated):
            s = {k: sem("e0_" + k) for k in (
                "x16",
                "w16",
                "up",
                "hidden",
                "low",
                "down",
                "added",
            )}
            w_in = [sem(f"e0_w_in{p}") for p in range(2)]
            x0 = x_steps[0]
            normed = CHUNKS * turns[0]
            U = CHUNKS * FT0
            TU = 2 * U
            LAG = 4
            BUFS = 8
            LOW_AHEAD, ADDED_AHEAD = 4, 2
            SCALE = 2.0 ** 8
            x_steps[0] += E0 * CHUNKS
            top[0] = body
            w1 = [take([F0]) for _ in range(2)]
            w2 = [take([FT0 * D]) for _ in range(2)]
            b1 = [take([FT0]) for _ in range(2)]
            w1_16 = [take([2, F0], F16) for _ in range(2)]
            w2_16 = [take([2, FT0 * D], F16) for _ in range(2)]
            x16 = take([2, B * S], F16)
            hid = take([4, CHUNK])
            hid16 = [take([BUFS, CHUNK], F16) for _ in range(2)]
            small_gates = take([TILES, EMAX])
            assert top[0] <= 36800
            PASSES = ((0, 0), (0, 1), (1, 0))

            def sync(sp):
                def load(i, p):
                    e = i * 2 + p
                    sp.dma_start(w1[p], io["w1"][bass.ds(e, 1)].rearrange("e p f -> p (e f)")).then_inc(w_in[p], 16)
                    sp.dma_start(w2[p], io["w2"][bass.ds(e, 1)].rearrange("e p t d -> p (e t d)")).then_inc(w_in[p], 16)
                    sp.dma_start(b1[p], io["b1"][bass.ds(e, 1)].rearrange("e p f -> p (e f)")).then_inc(w_in[p], 16)
                wait(sp, x_done, nonlocal_x[0])
                load(0, 0)
                load(0, 1)
                with sp.Fori(1, E0 // 2) as i:
                    for p in range(2):
                        wait_alone(sp, s["down"], i * TU - TU + (p + 1) * U, sp_step)
                        load(i, p)

            def pool(g):
                g.sem_inc(s["low"], LOW_AHEAD)
                g.wait_ge(nrm_xt, normed)
                for k in range(CHUNKS):
                    c = slice(k * CHUNK, (k + 1) * CHUNK)
                    g.tensor_copy(x16[:, 0, c], xn_t[:, c]).then_inc(s["x16"], 1)
                    g.wait_ge(s["x16"], 2 * k + 1)
                    g.tensor_tensor(x16[:, 1, c], xn_t[:, c], x16[:, 0, c], ALU.subtract).then_inc(s["x16"], 1)
                with g.Fori(0, E0 // 2) as i:
                    for u in range(TU):
                        g.wait_ge(s["hidden"], i * TU + u + 1)
                        g.tensor_tensor(hid16[1][:, u % BUFS, :], hid[:, u % 4, :], hid16[0][:, u % BUFS, :], ALU.subtract)\
                         .then_inc(s["low"], 1)

            def tensor(pe):
                pe.wait_ge(x_done, x0)
                pe.wait_ge(g_t, gated)
                pe.wait_ge(s["x16"], 2 * CHUNKS)

                def up(i, u):
                    if u >= TU:
                        i, u = i + 1, u - TU
                    p, c, f = u // U, u // FT0 % CHUNKS, u % FT0
                    if u % U == 0:
                        pe.wait_ge(s["w16"], i * 2 + p + 1)
                    if not (isinstance(i, int) and i == 0 and u < 4):
                        pe.wait_ge(s["hidden"], i * TU + u - 3)
                    for k, (w, xk) in enumerate(PASSES):
                        last = pe.matmul(bank[u % 4][:, :], w1_16[p][:, w, f * P:(f + 1) * P],
                                         x16[:, xk, c * CHUNK:(c + 1) * CHUNK], start=k == 0, stop=k == 2)
                    last.then_inc(s["up"], 1)

                def down(i, u):
                    p, f = u // U, u % FT0
                    out_no = u // FT0
                    pe.wait_ge(s["low"], i * TU + u + 1 + LOW_AHEAD)
                    if f == 0:
                        pe.wait_ge(s["added"], i * 2 * CHUNKS + out_no - 1 + ADDED_AHEAD)
                    for j in range(CT):
                        for k, (h, w) in enumerate(PASSES):
                            last = pe.matmul(bank[4 + out_no % 2][:, j * P:(j + 1) * P],
                                             hid16[h][:, u % BUFS, j * P:(j + 1) * P],
                                             w2_16[p][:, w, f * D:(f + 1) * D],
                                             start=f == 0 and j == 0 and k == 0, stop=f == FT0 - 1 and k == 2,
                                             skip_group_check=True)
                    last.then_inc(s["down"], 1)

                for u in range(LAG):
                    up(0, u)
                with pe.Fori(0, E0 // 2 - 1) as i:
                    for u in range(TU):
                        up(i, u + LAG)
                        down(i, u)
                for u in range(TU):
                    if u + LAG < TU:
                        up(E0 // 2 - 1, u + LAG)
                    down(E0 // 2 - 1, u)

            def scalar(act):
                with act.Fori(0, E0 // 2) as i:
                    for u in range(TU):
                        if u % U == 0:
                            act.wait_ge(w_in[u // U], i * 48 + 48)
                        act.wait_ge(s["up"], i * TU + u + 1)
                        act.wait_ge(s["low"], i * TU + u - 3 + LOW_AHEAD)
                        for to in (hid[:, u % 4, :], hid16[0][:, u % BUFS, :]):
                            last = act.activation(to, bank[u % 4][:, :], ACT.Gelu, bias=b1[u // U][:, u % FT0:u % FT0 + 1],
                                                  scale=1 / SCALE)
                        last.then_inc(s["hidden"], 1)

            def vector(v):
                c = dve(v)

                def split_weights(i, p):
                    v.wait_ge(w_in[p], i * 48 + 48)
                    v.tensor_scalar(w1_16[p][:, 0, :], w1[p], SCALE, None, ALU.mult)
                    c.step(v.tensor_scalar(w2_16[p][:, 0, :], w2[p], SCALE, None, ALU.mult)).settle()
                    v.scalar_tensor_tensor(w1_16[p][:, 1, :], w1[p], SCALE, w1_16[p][:, 0, :], ALU.mult, ALU.subtract)
                    v.scalar_tensor_tensor(w2_16[p][:, 1, :], w2[p], SCALE, w2_16[p][:, 0, :], ALU.mult, ALU.subtract)\
                     .then_inc(s["w16"], 1)

                def turn(i, last_turn):
                    for n in range(2 * CHUNKS):
                        p, k = divmod(n, CHUNKS)
                        v.wait_ge(s["down"], i * TU + (n + 1) * FT0)
                        v.wait_ge(x_done, i * 2 * CHUNKS + n + x0)
                        for j in range(CT):
                            t = CT * k + j
                            last = v.scalar_tensor_tensor(x[:, t, :], bank[4 + n % 2][:, j * P:(j + 1) * P],
                                                          small_gates[:, t, bass.ds(i * 2 + p, 1)], x[:, t, :],
                                                          ALU.mult, ALU.add)
                        last.then_inc(x_done, 1)
                        v.wait_ge(x_done, i * 2 * CHUNKS + n + 1 + x0)
                        v.sem_inc(s["added"], 1)
                        if k == 0 and not (last_turn and p):
                            split_weights(i + p, 1 - p)

                v.sem_inc(s["added"], ADDED_AHEAD)
                split_weights(0, 0)
                c.step(v.tensor_scalar(small_gates, gates, 1 / SCALE, None, ALU.mult)).settle()
                v.wait_ge(x_done, x0)
                with v.Fori(0, E0 // 2 - 1) as i:
                    c.turn(i, 2)
                    turn(i, False)
                    c.turned(E0 // 2 - 1)
                turn(E0 // 2 - 1, True)

            programs["sync"].append(sync)
            programs["gpsimd"].append(pool)
            programs["tensor"].append(tensor)
            programs["scalar"].append(scalar)
            programs["vector"].append(vector)

        def feed_forward(layer, waits):
            s = {k: sem(f"f{layer}_" + k) for k in (
                "inner",
                "acted",
                "hidden",
                "down",
                "x16",
                "w16",
            )}
            x0 = x_steps[0]
            normed = CHUNKS * turns[0]
            x_steps[0] += CHUNKS
            top[0] = body
            E = (0, E1, E2, 0)[layer]
            routed = E // 2
            NT = (0, 5, 10, 4)[layer]
            K = 5 if layer == 1 else 4
            acted = take([K, CHUNK])
            hid = take([K, CHUNK])
            if layer == 3:
                fc_t = take([F0])
                proj_t = take([4, D])
                fc_e = take([4, D])
                proj_e = take([F0])
                tern = take([F0])
                scale = take([8])
                low = take([F0])
                made = sem("f3_made")
                made_pe = sem("f3_made_pe")
                stored = sem("stored")
                wg, wd = fc_t, proj_t
            else:
                wg, wu, wd = (far[f"w{c}{layer}"] for c in "gud")
                spread = expert1 if layer == 1 else far["expert"]
                SCALE = 2.0 ** 8
                NU = wu.shape[1]
                x16 = take([2, B * S], F16)
                wg16, wu16 = take([2, NT * P], F16), take([2, NU * P], F16)
                spread16 = take([2, routed * P], F16)
                gates16 = take([2, B * S], F16)
                SPREAD_PASSES = ((0, 0), (1, 0)) if layer == 1 else ((0, 0), (0, 1))

            def pool(g):
                g.wait_ge(nrm_xt, normed)
                for k in range(CHUNKS):
                    c = slice(k * CHUNK, (k + 1) * CHUNK)
                    g.tensor_copy(x16[:, 0, c], xn_t[:, c]).then_inc(s["x16"], 1)
                    g.wait_ge(s["x16"], 2 * k + 1)
                    g.tensor_tensor(x16[:, 1, c], xn_t[:, c], x16[:, 0, c], ALU.subtract).then_inc(s["x16"], 1)

            def split_operands(v, c):
                for w, to in ((wg, wg16), (wu, wu16)):
                    flat = w.rearrange("p t c -> p (t c)")
                    c.step(v.tensor_scalar(to[:, 0, :], flat, SCALE, None, ALU.mult)).settle()
                    v.scalar_tensor_tensor(to[:, 1, :], flat, SCALE, to[:, 0, :], ALU.mult, ALU.subtract)
                for q, n in waits:
                    v.wait_ge(q, n)
                flat = spread[0:E, 0:routed, :].rearrange("p t c -> p (t c)")
                c.step(v.tensor_copy(spread16[0:E, 0, :], flat))
                c.step(v.tensor_copy(gates16[0:E, 0, :], gates_t[0:E, :])).settle()
                if layer == 1:
                    last = v.tensor_tensor(spread16[0:E, 1, :], flat, spread16[0:E, 0, :], ALU.subtract)
                else:
                    last = v.tensor_tensor(gates16[0:E, 1, :], gates_t[0:E, :], gates16[0:E, 0, :], ALU.subtract)
                last.then_inc(s["w16"], 1)

            def up_of(t):
                return layer == 1 or (layer == 2 and t >= routed)

            def gated(t):
                return t < routed

            def tensor(pe):
                pe.sem_inc(s["down"], K)
                pe.wait_ge(x_done, x0)
                for q, n in waits:
                    pe.wait_ge(q, n)
                if layer < 3:
                    pe.wait_ge(s["w16"], 1)
                    pe.wait_ge(s["x16"], 2 * CHUNKS)
                if layer == 3:
                    pe.matmul(bank[0][0:16, :], far["fast_b"][0:16, :], far["u_t"][0:16, :], start=True, stop=True)\
                      .then_inc(made_pe, 1)
                    pe.wait_ge(made, 1)
                    pe.matmul(bank[1][:, :], far["v"][0:16, :], low[0:16, :], start=True, stop=True).then_inc(made_pe, 1)
                    pe.wait_ge(made, 3)
                    for t in range(4):
                        pe.transpose(bank[2][:, t * P:(t + 1) * P], fc_e[:, t, :], eye)
                        last = pe.transpose(bank[3][:, t * P:(t + 1) * P], proj_e[:, t * P:(t + 1) * P], eye)
                    last.then_inc(made_pe, 1)
                    pe.wait_ge(made, 5)

                with pe.Fori(0, CHUNKS // 2) as i:
                    def inner(u):
                        p, t = divmod(u, NT)
                        if u >= 2:
                            pe.wait_ge(s["hidden"], i * 2 * NT + u - 1 + K)
                        cols = bass.ds((i * 2 + p) * CHUNK, CHUNK)
                        if layer == 3:
                            last = pe.matmul(bank[u % 2][:, :], wg[:, t * P:(t + 1) * P], xn_t[:, cols], start=True, stop=True)
                        else:
                            tu = t - (routed if layer == 2 else 0)
                            for b0, w16, at in ((0, wg16, t), (2, wu16, tu)):
                                if b0 and not up_of(t):
                                    continue
                                for k, (w, xk) in enumerate(((0, 0), (0, 1), (1, 0))):
                                    last = pe.matmul(bank[b0 + u % 2][:, :], w16[:, w, at * P:(at + 1) * P],
                                                     x16[:, xk, cols], start=k == 0, stop=k == 2)
                        if gated(t):
                            for k, (w, gk) in enumerate(SPREAD_PASSES):
                                last = pe.matmul(bank[4 + u % 2][:, :], spread16[0:E, w, t * P:(t + 1) * P],
                                                 gates16[0:E, gk, cols], start=k == 0, stop=k == 1)
                        last.then_inc(s["inner"], 1)

                    def down(u):
                        p, t = divmod(u, NT)
                        pe.wait_ge(s["hidden"], i * 2 * NT + u + 1 + K)
                        if t == 0:
                            pe.wait_ge(x_done, i * 2 + x0)
                        for j in range(CT):
                            last = pe.matmul(bank[6 + p][:, j * P:(j + 1) * P], hid[:, u % K, j * P:(j + 1) * P],
                                             wd[:, t, :], start=t == 0 and j == 0, stop=t == NT - 1,
                                             skip_group_check=True)
                        last.then_inc(s["down"], 1)

                    for u in range(2 * NT + 1):
                        if u < 2 * NT:
                            inner(u)
                        if u >= 1:
                            down(u - 1)

            def scalar(act):
                with act.Fori(0, CHUNKS // 2) as i:
                    for u in range(2 * NT):
                        act.wait_ge(s["inner"], i * 2 * NT + u + 1)
                        act.wait_ge(s["hidden"], i * 2 * NT + u + 1)
                        act.activation(acted[:, u % K, :], bank[u % 2][:, :], ACT.Relu if layer == 3 else ACT.Silu,
                                       scale=1.0 if layer == 3 else 1 / SCALE)\
                           .then_inc(s["acted"], 1)

            def vector(v):
                c = dve(v)
                v.sem_inc(s["hidden"], K)
                if layer == 3:
                    v.wait_ge(made_pe, 1)
                    v.tensor_copy(low[0:16, :], bank[0][0:16, :]).then_inc(made, 1)
                    for n, (w, to, shape) in enumerate(((far["w_fc"], fc_e, 4), (far["w_proj"], proj_e, 1))):
                        w3 = w if n == 0 else w.unsqueeze(1)
                        size = D if n == 0 else F0
                        t3 = tern.rearrange("p (a b) -> p a b", b=size)
                        to3 = to if n == 0 else to.unsqueeze(1)
                        sc, rc = scale[:, 0:shape], scale[:, 4:4 + shape]
                        wide = [P, shape, size]
                        c.step(v.scalar_tensor_tensor(t3, w3, -1.0, w3, ALU.mult, ALU.max)).settle()
                        c.step(v.tensor_reduce(sc, t3, AX.X, ALU.add)).settle()
                        c.step(v.tensor_scalar(sc, sc, 1.0 / size, 1e-5, ALU.mult, ALU.max)).settle()
                        c.step(v.reciprocal(rc, sc)).settle()
                        c.step(v.tensor_tensor(t3, w3, rc.unsqueeze(2).to_broadcast(wide), ALU.mult)).settle()
                        c.step(v.tensor_scalar(t3, t3, -1.0, 1.0, ALU.max, ALU.min)).settle()
                        c.step(v.tensor_scalar(t3, t3, ROUND, ROUND, ALU.add, ALU.subtract)).settle()
                        c.step(v.tensor_tensor(t3, t3, w3, ALU.subtract)).settle()
                        c.step(v.tensor_tensor(t3, w3, t3, ALU.add)).settle()
                        v.tensor_tensor(to3, t3, sc.unsqueeze(2).to_broadcast(wide), ALU.mult).then_inc(made, 1)
                        v.wait_ge(made, n + 2)
                    v.wait_ge(made_pe, 3)
                    v.wait_ge(made, 3)
                    v.tensor_copy(proj_t, bank[3][:, :].rearrange("p (t d) -> p t d", d=D)).then_inc(made, 1)
                    c.step(v.tensor_copy(tern, bank[2][:, :])).settle()
                    v.scalar_tensor_tensor(fc_t, bank[1][:, :], far["gate"][:, 0:1], tern, ALU.mult, ALU.add)\
                     .then_inc(made, 1)
                if layer < 3:
                    split_operands(v, c)
                with v.Fori(0, CHUNKS // 2) as i:
                    c.turn(i, 2 * (routed if layer == 1 else 0))
                    for u in range(2 * NT):
                        p, t = divmod(u, NT)
                        v.wait_ge(s["acted"], i * 2 * NT + u + 1)
                        v.wait_ge(s["down"], i * 2 * NT + u + 1)
                        a, h = acted[:, u % K, :], hid[:, u % K, :]
                        if layer == 3:
                            last = v.tensor_tensor(h, a, a, ALU.mult)
                        elif up_of(t) and gated(t):
                            c.step(v.scalar_tensor_tensor(h, bank[2 + u % 2][:, :], 1 / SCALE, a, ALU.mult, ALU.mult)).settle()
                            last = v.tensor_tensor(h, h, bank[4 + u % 2][:, :], ALU.mult)
                        elif gated(t):
                            last = v.tensor_tensor(h, a, bank[4 + u % 2][:, :], ALU.mult)
                        else:
                            last = v.scalar_tensor_tensor(h, bank[2 + u % 2][:, :], 1 / SCALE, a, ALU.mult, ALU.mult)
                        last.then_inc(s["hidden"], 1)
                        if t == 0 and p == 1:
                            add(v, i, 0)
                    add(v, i, 1)
                    c.turned(CHUNKS // 2)

            def add(v, i, p):
                v.wait_ge(s["down"], i * 2 * NT + (p + 1) * NT + K)
                xs = x[:, bass.ds((i * 2 + p) * CT, CT), :]
                v.tensor_tensor(xs, bank[6 + p][:, :].rearrange("p (t d) -> p t d", d=D), xs, ALU.add).then_inc(x_done, 1)

            def sync(sp):
                with sp.Fori(0, CHUNKS) as i:
                    wait_alone(sp, x_done, i + 1 + x0, sp_step)
                    sp.dma_start(out[:, bass.ds(i * CT, CT), :], x[:, bass.ds(i * CT, CT), :]).then_inc(stored, 16)
                sp.wait_ge(stored, 16 * CHUNKS)

            programs["tensor"].append(tensor)
            programs["scalar"].append(scalar)
            programs["vector"].append(vector)
            if layer < 3:
                programs["gpsimd"].append(pool)
            if layer == 3:
                programs["sync"].append(sync)

        def retention():
            s = {k: sem("r_" + k) for k in (
                "rotated",
                "turned",
                "spread",
                "scored",
                "masked",
                "mixed",
                "state",
                "kept",
                "output",
                "ready",
            )}
            c_in = [sem(f"r_c_in{p}") for p in range(2)]
            x0 = x_steps[0]
            x_steps[0] += B
            normed = CHUNKS * norms[0]
            top[0] = body
            tok = [take([SB, D]) for _ in range(2)]
            qk = [take([2, SB, D]) for _ in range(2)]
            turn_a = take([2, SB, D])
            turn_b = take([2, SB, D])
            k_t = [take([S]) for _ in range(2)]
            q_t = [take([S]) for _ in range(2)]
            q_own = [take([H, S]) for _ in range(2)]
            v_own = [take([SB, H * D + 8 * H]) for _ in range(2)]
            prob = take([3, HG, P])
            kept = take([P])
            assert top[0] <= 36800
            turn = far["turn"].rearrange("p (k t d) -> p k t d", k=4, d=D)
            UNITS = SB * GROUPS

            def plan_r(first, last):
                for u in range(UNITS):
                    yield "scores", 0, u
                    if u >= 1:
                        yield "mix", 0, u - 1
                    if u == 1 and not last:
                        yield "rotate", 1, 0
                    if u == 2:
                        yield "state", 0, 0
                    if u == 4 and not last:
                        yield "turn", 1, 0
                    if u == 1 and not first:
                        yield "add", -1, 0
                yield "mix", 0, UNITS - 1
                yield "inter", 0, 0

            def walk_r(eng, steps, chain=None):
                def go(order, at):
                    for name, ahead, u in order:
                        if name in steps:
                            steps[name](eng, at.move(ahead), u)
                go([("rotate", 0, 0), ("turn", 0, 0)], Seq(0, 0))
                go(plan_r(True, False), Seq(0, 0))
                with eng.Fori(0, B // 2 - 1) as i:
                    if chain:
                        chain.turn(i, steps["chained"])
                    go(plan_r(False, False), Seq(i, 1))
                    go(plan_r(False, False), Seq(i + 1, 0))
                    if chain:
                        chain.turned(B // 2 - 1)
                go(plan_r(False, True), Seq(B // 2 - 1, 1))
                go([("add", 0, 0)], Seq(B // 2 - 1, 1))

            def sync(sp):
                wait(sp, x_done, x0)

                def load(i, p):
                    sp.dma_start(tok[p], io["ctx"][:, bass.ds((i * 2 + p) * SB, SB), :]).then_inc(c_in[p], 16)
                load(0, 0)
                load(0, 1)
                with sp.Fori(1, B // 2) as i:
                    for p in range(2):
                        wait_alone(sp, s["state"], i * 2 + p - 1, sp_step)
                        wait_alone(sp, s["spread"], i * 2 + p - 1, sp_step)
                        load(i, p)

            def pool(g):
                g.wait_ge(x_done, x0)
                for p in range(2):
                    g.memset(v_own[p], 0.0).then_inc(s["ready"], 1)

            def tensor(pe):
                def turn_pe(pe, q, _):
                    pe.wait_ge(s["rotated"], q.b + 1)
                    wait(pe, s["spread"], q.b)
                    for k in range(2):
                        for t in range(SB):
                            last = pe.transpose(bank[2][:, k * S + t * P:k * S + (t + 1) * P], qk[q.p][:, k, t, :], eye)
                    last.then_inc(s["turned"], 1)

                def scores(pe, q, u):
                    t, g = divmod(u, GROUPS)
                    if u == 0:
                        pe.wait_ge(s["spread"], q.b + 1)
                    wait(pe, s["masked"], q.b * UNITS + u - 1)
                    pe.matmul(bank[u % 2][:, :], k_t[q.p][:, t * P:(t + 1) * P],
                              q_own[q.p][:, HG * g:HG * g + HG, t * P:(t + 1) * P], start=True, stop=True)\
                      .then_inc(s["scored"], 1)

                def mix(pe, q, u):
                    t, g = divmod(u, GROUPS)
                    pe.wait_ge(s["masked"], q.b * UNITS + u + 1)
                    if u == 0:
                        wait(pe, x_done, q.b - 1 + x0)
                    for j in range(HG):
                        h = HG * g + j
                        last = pe.matmul(bank[4 + q.p][:, t * P:(t + 1) * P], prob[:, u % 3, j, :],
                                         v_own[q.p][:, t, h * D:(h + 1) * D], start=u == 0 and j == 0,
                                         stop=g == GROUPS - 1 and j == HG - 1 and t == 0, skip_group_check=True)
                    last.then_inc(s["mixed"], 1)

                def state(pe, q, _):
                    pe.wait_ge(s["rotated"], q.b + 1)
                    wait(pe, s["kept"], q.b)
                    pe.matmul(bank[3][:, 0:P], qk[q.p][:, 1, 0, :], tok[q.p][:, 0, :], start=True, stop=True)\
                      .then_inc(s["state"], 1)

                def inter(pe, q, _):
                    pe.wait_ge(s["kept"], q.b + 1)
                    pe.matmul(bank[4 + q.p][:, P:2 * P], q_t[q.p][:, P:2 * P], kept, start=False, stop=True,
                              skip_group_check=True).then_inc(s["output"], 1)

                walk_r(pe, {"turn": turn_pe, "scores": scores, "mix": mix, "state": state, "inter": inter})

            def scalar(act):
                act.wait_ge(far_in, 16 * FAR_LOADS)
                act.wait_ge(s["ready"], 2)

                def turn_act(act, q, _):
                    act.wait_ge(s["turned"], q.b + 1)
                    wait(act, s["output"], q.b - 1)
                    act.activation(k_t[q.p], bank[2][:, S:2 * S], ACT.Copy)
                    act.activation(q_t[q.p], bank[2][:, 0:S], ACT.Copy)
                    for t in range(SB):
                        act.activation(v_own[q.p][:, t, 0:H * (D + DH)].rearrange("p (h c) -> p h c", c=D + DH)[:, :, 0:DH],
                                       tok[q.p][:, t, :].rearrange("p (h d) -> p h d", d=DH), ACT.Copy)
                    for h in range(H):
                        last = act.activation(q_own[q.p][:, h, :], bank[2][:, 0:S], ACT.Copy, scale=far["own"][:, h:h + 1])
                    last.then_inc(s["spread"], 1)

                walk_r(act, {"turn": turn_act})

            def vector(v):
                c = dve(v)
                v.wait_ge(far_in, 16 * FAR_LOADS)
                v.wait_ge(nrm_xn, normed)

                def rotate(v, q, _):
                    v.wait_ge(c_in[q.p], q.i * 16 + 16)
                    wait(v, s["state"], q.b - 1)
                    for k in range(2):
                        src = tok[q.p] if k else xn[:, bass.ds(q.b * SB, SB), :]
                        pair = src.rearrange("p t (n two) -> p t n two", two=2)
                        ta, tb = turn_a[:, k], turn_b[:, k].rearrange("p t (n two) -> p t n two", two=2)
                        sn = turn[:, 2 * k + 1].rearrange("p t (n two) -> p t n two", two=2)
                        v.tensor_tensor(ta, src, turn[:, 2 * k], ALU.mult)
                        v.tensor_tensor(tb[:, :, :, 0], pair[:, :, :, 1], sn[:, :, :, 0], ALU.mult)
                        c.step(v.tensor_tensor(tb[:, :, :, 1], pair[:, :, :, 0], sn[:, :, :, 1], ALU.mult)).settle()
                        last = v.tensor_tensor(qk[q.p][:, k], ta, turn_b[:, k], ALU.add)
                    last.then_inc(s["rotated"], 1)

                def scores(v, q, u):
                    v.wait_ge(s["scored"], q.b * UNITS + u + 1)
                    wait(v, s["mixed"], q.b * UNITS + u - 2)
                    v.tensor_tensor(prob[:, u % 3], bank[u % 2][:, :].rearrange("p (h c) -> p h c", c=P),
                                    far["causal"].unsqueeze(1).to_broadcast([P, HG, P]), ALU.mult).then_inc(s["masked"], 1)

                def state(v, q, _):
                    v.wait_ge(s["state"], q.b + 1)
                    wait(v, s["output"], q.b)
                    v.tensor_tensor(kept, bank[3][:, 0:P], far["block"], ALU.mult).then_inc(s["kept"], 1)

                def add(v, q, _):
                    v.wait_ge(s["output"], q.b + 1)
                    xs = x[:, bass.ds(q.b * SB, SB), :]
                    v.tensor_tensor(xs, bank[4 + q.p][:, 0:S].rearrange("p (t d) -> p t d", d=D), xs, ALU.add)\
                     .then_inc(x_done, 1)

                walk_r(v, {"rotate": rotate, "scores": scores, "state": state, "add": add, "chained": 4}, c)

            programs["sync"].append(sync)
            programs["gpsimd"].append(pool)
            programs["tensor"].append(tensor)
            programs["scalar"].append(scalar)
            programs["vector"].append(vector)

        def sublayers():
            norm(0)
            attention(0, turns[0])
            yield
            nonlocal_x[0] = x_steps[0]
            programs["sync"].append(far_sync)
            norm(1)
            experts0(gate(0))
            yield
            norm(2)
            attention(1, turns[0])
            yield
            norm(3)
            feed_forward(1, [(g_t, gate(1)), (g_const, 2)])
            yield
            norm(4, need_t=False)
            retention()
            yield
            norm(5)
            feed_forward(2, [(g_t, gate(2))])
            yield
            norm(6)
            attention(3, turns[0])
            yield
            norm(7)
            feed_forward(3, [(nrm_xt, CHUNKS * turns[0])])
            yield

        for n, _ in enumerate(sublayers()):
            if n + 1 == upto:
                break

        block = ctx.enter_context(nc.Block())

        @block.sync
        def _(sp):
            for part in programs["sync"]:
                part(sp)

        @block.gpsimd
        def _(g):
            for part in programs["gpsimd"]:
                part(g)

        @block.scalar
        def _(act):
            for part in programs["scalar"]:
                part(act)

        @block.vector
        def _(v):
            for part in programs["vector"]:
                part(v)

        @block.tensor
        def _(pe):
            for part in programs["tensor"]:
                part(pe)


def laid_out(a):
    f = {k: np.ascontiguousarray(v) for k, v in a.items()}
    r = {}
    r["x"] = f["x"].reshape(TILES, P, D).transpose(1, 0, 2)
    r["ctx_t"] = f["ctx_1024"].reshape(B * S, D).T
    r["ctx"] = f["ctx_1024"].reshape(TILES, P, D).transpose(1, 0, 2)
    r["mask0_q"] = f["mask_BxSxS2_bk0"]
    r["mask0_t"] = f["mask_BxSxS2_bk0"].transpose(0, 2, 1)
    r["mask1_q"] = f["mask_Bx1xSxS2_ik1"][:, 0]
    r["mask1_t"] = r["mask1_q"].transpose(0, 2, 1)
    r["bias1_q"] = f["fside_BxSxS2_0"]
    r["bias1_t"] = r["bias1_q"].transpose(0, 2, 1)
    r["bias0_q"] = f["L0_xattn_position_bias"]
    r["bias0_t"] = r["bias0_q"].transpose(0, 2, 1)
    for n in ("mask0_q", "mask0_t", "mask1_q", "mask1_t", "bias1_q", "bias1_t"):
        r[n] = r[n].reshape(B, SB, P, S).transpose(0, 2, 1, 3).reshape(B, P, SB * S)
    for n in ("bias0_q", "bias0_t"):
        r[n] = r[n].reshape(H, SB, P, S).transpose(2, 0, 1, 3).reshape(P, H, SB * S)
    for n, c in (("wq0", "q"), ("wk0", "k"), ("wv0", "v")):
        r[n] = f[f"L0_xattn_W{c}"].T
    r["wo0"] = f["L0_xattn_Wo"].T.reshape(PAIRS, P, D).transpose(1, 0, 2)
    r["keys_t"], r["rw_t"] = f["L0_ffn_keys"].T, f["L0_ffn_rw"].T
    r["rb"], r["b2"] = f["L0_ffn_rb"][None], f["L0_ffn_b2"]
    r["w1"] = f["L0_ffn_w1"].transpose(0, 2, 1)
    r["b1"] = f["L0_ffn_b1"].reshape(E0, FT0, P).transpose(0, 2, 1)
    r["w2"] = f["L0_ffn_w2"].transpose(0, 2, 1).reshape(E0, FT0, P, D).transpose(0, 2, 1, 3)
    rows = (HG * np.arange(GROUPS)[:, None, None] + np.arange(HG)[None, :, None]) * DH + np.arange(32)[None, None] % DH
    rows = rows.reshape(GROUPS, P)
    for n in (1, 3):
        for c in "qk":
            r[f"w{c}{n}"] = f[f"L{n}_xattn_W{c}"].T[:, rows]
            r[f"b{c}{n}"] = f[f"L{n}_xattn_b{c}"][rows].T
        for c in "vo":
            r[f"w{c}{n}"] = f[f"L{n}_xattn_W{c}"].T
            r[f"b{c}{n}"] = f[f"L{n}_xattn_b{c}"][None]
    r["gate1"], r["lb1"] = f["L1_ffn_gate_w"].T, f["L1_ffn_lb_bias"][None]
    for n, c in (("wg1", "gate"), ("wu1", "up")):
        w = np.concatenate([f[f"L1_ffn_expert_{c}_w"].reshape(E1 // 2, P, D), f[f"L1_ffn_shared_{c}_w"][None]])
        r[n] = w.transpose(2, 0, 1)
    w = np.concatenate([f["L1_ffn_expert_down_w"].transpose(0, 2, 1).reshape(E1 // 2, P, D),
                        f["L1_ffn_shared_down_w"].T[None]])
    r["wd1"] = w.transpose(1, 0, 2)
    r["gate2"] = f["L2_ffn_gate_w"].T
    w = np.concatenate([f["L2_ffn_w1"].reshape(E2 // 2, P, D), f["L2_ffn_sfc1"].reshape(2, P, D)])
    r["wg2"] = w.transpose(2, 0, 1)
    r["wu2"] = f["L2_ffn_sfc2"].reshape(2, P, D).transpose(2, 0, 1)
    w = np.concatenate([f["L2_ffn_w2"].transpose(0, 2, 1).reshape(E2 // 2, P, D), f["L2_ffn_sfc3"].T.reshape(2, P, D)])
    r["wd2"] = w.transpose(1, 0, 2)
    r["w_fc"] = f["L3_ffn_w_fc"].reshape(4, P, D).transpose(1, 0, 2)
    r["w_proj"] = f["L3_ffn_w_proj"]
    r["u_t"], r["v"], r["fast_b"] = f["L3_ffn_u"].T, f["L3_ffn_v"], f["L3_ffn_fast_b"]
    r["gate"] = np.broadcast_to(f["L3_ffn_gate"].reshape(1, 1), (P, 1))
    for n, c in shape_constants().items():
        r[n] = c.astype(np.float32)
    for n in ("at", "expert", "causal", "own", "block", "turn"):
        r[n] = r.pop("c_" + n)
    r["turn"] = r["turn"].reshape(P, -1)
    return {n: np.ascontiguousarray(v) for n, v in r.items()}


def kernel(**inputs):
    import concourse.bacc as bacc
    from concourse.bass_utils import run_bass_kernel_spmd

    arrays = laid_out({k: np.asarray(v) for k, v in inputs.items()})
    nc = bacc.Bacc("TRN2", target_bir_lowering=False, num_devices=1)
    io = {n: nc.dram_tensor(n, a.shape, mybir.dt.from_np(a.dtype), kind="ExternalInput").ap()
          for n, a in arrays.items()}
    out = nc.dram_tensor("out", (P, TILES, D), F32, kind="ExternalOutput").ap()
    build(nc, io, out)
    r = run_bass_kernel_spmd(nc, [arrays], core_ids=[0])
    return np.ascontiguousarray(r.results[0]["out"].transpose(1, 0, 2).reshape(B, S, D))
```
